# Optimizing a Trainium2 kernel written in Bass

```python
import numpy as np
import jax
import jax.numpy as jnp

def _softmax(x, axis=-1):
    return jax.nn.softmax(x, axis=axis)

def _gelu(x):
    return jax.nn.gelu(x, approximate=True)

def _silu(x):
    return jax.nn.silu(x)

def _sigmoid(x):
    return jax.nn.sigmoid(x)

def _layernorm(x, axis=-1, eps=1e-05):
    m = jnp.mean(x, axis=axis, keepdims=True)
    v = jnp.var(x, axis=axis, keepdims=True)
    return (x - m) / jnp.sqrt(v + eps)

def _scatter_add(tgt, idx, src, axis=0):
    return tgt.at[idx].add(src)

def _segment_sum(src, seg, n):
    return jax.ops.segment_sum(src, seg, n)
kernel_name = 'mk_gnn_resnorm_d2_gnn_r8_27842c'

def setup_inputs(seed: int=0):
    np.random.seed(seed)
    _w = jnp.asarray

    def _rec_inputs():
        import jax
        import jax.numpy as jnp
        _gk = jax.random.key(seed)
        x = -0.0001006 + 1 * jax.random.normal(jax.random.fold_in(_gk, 1), (12500, 96), jnp.float32)
        src = jax.random.randint(jax.random.fold_in(_gk, 2), (200000,), 0, 12500, jnp.int32)
        dst = jax.random.randint(jax.random.fold_in(_gk, 3), (200000,), 0, 12500, jnp.int32)
        _o = jnp.argsort(dst, stable=True)
        src = src[_o]
        dst = dst[_o]
        edge_attr_17 = jax.random.uniform(jax.random.fold_in(_gk, 12), (200000, 17), jnp.float32, 0.0, 1)
        return (x, src, dst, edge_attr_17)
    x, src, dst, edge_attr_17 = _rec_inputs()

    def _L0_gnn_setup():
        import jax, jax.numpy as jnp
        import numpy as np
        N = 6250
        E = 100000
        D = 96
        ED = 17
        key = jax.random.key(seed)
        ks = jax.random.split(key, 12)
        x = jax.random.normal(ks[0], (N, D), dtype=jnp.float32)
        edge_index = jax.random.randint(ks[1], (2, E), 0, N, dtype=jnp.int64)
        edge_attr = jax.random.uniform(ks[2], (E, ED), dtype=jnp.float32)
        s = 1.0 / np.sqrt(ED)
        W1 = jax.random.uniform(ks[3], (D, ED), jnp.float32, -s, s)
        b1 = jax.random.uniform(ks[4], (D,), jnp.float32, -s, s)
        s = 1.0 / np.sqrt(D)
        W2 = jax.random.uniform(ks[5], (D, D), jnp.float32, -s, s)
        b2 = jax.random.uniform(ks[6], (D,), jnp.float32, -s, s)
        Ws = jax.random.uniform(ks[7], (D, D), jnp.float32, -s, s)
        bs = jax.random.uniform(ks[8], (D,), jnp.float32, -s, s)
        Wn = jax.random.uniform(ks[9], (D, D), jnp.float32, -s, s)
        bn = jax.random.uniform(ks[10], (D,), jnp.float32, -s, s)
        return {'x': x, 'edge_index': edge_index, 'edge_attr': edge_attr, 'W1': W1, 'b1': b1, 'W2': W2, 'b2': b2, 'Ws': Ws, 'bs': bs, 'Wn': Wn, 'bn': bn}
    _L0_gnn_all = _L0_gnn_setup()
    _L0_gnn_in = {k: v for k, v in _L0_gnn_all.items() if k in ('W1', 'b1', 'W2', 'b2', 'Ws', 'bs', 'Wn', 'bn')}
    del _L0_gnn_all

    def _L1_gnn_setup():
        import jax, jax.numpy as jnp
        import numpy as np
        N_NODES = 6250
        N_EDGES = 100000
        D_IN = 96
        D_HID = 96
        D_OUT = 96
        EPS = 1e-12

        def _sage_pool_layer(x, src, dst, Wp, bp, Ws, Wn, b, n_nodes):
            m = jax.nn.relu(x @ Wp + bp)
            msgs = m[src]
            agg = jax.ops.segment_max(msgs, dst, num_segments=n_nodes)
            agg = jnp.where(jnp.isfinite(agg), agg, 0.0)
            return x @ Ws + agg @ Wn + b

        def _l2norm(h):
            n = jnp.linalg.norm(h, axis=1, keepdims=True)
            return h / jnp.maximum(n, EPS)
        key = jax.random.key(seed)
        ks = jax.random.split(key, 16)
        x = jax.random.normal(ks[0], (N_NODES, D_IN), dtype=jnp.float32)
        src = jax.random.randint(ks[1], (N_EDGES,), 0, N_NODES)
        dst = jax.random.randint(ks[2], (N_EDGES,), 0, N_NODES)
        s = 1.0 / np.sqrt(D_IN)
        return {'x': x, 'src': src, 'dst': dst, 'Wp1': jax.random.normal(ks[3], (D_IN, D_IN), dtype=jnp.float32) * s, 'bp1': jnp.zeros((D_IN,), jnp.float32), 'Ws1': jax.random.normal(ks[4], (D_IN, D_HID), dtype=jnp.float32) * s, 'Wn1': jax.random.normal(ks[5], (D_IN, D_HID), dtype=jnp.float32) * s, 'b1': jnp.zeros((D_HID,), jnp.float32), 'Wp2': jax.random.normal(ks[6], (D_HID, D_HID), dtype=jnp.float32) * s, 'bp2': jnp.zeros((D_HID,), jnp.float32), 'Ws2': jax.random.normal(ks[7], (D_HID, D_OUT), dtype=jnp.float32) * s, 'Wn2': jax.random.normal(ks[8], (D_HID, D_OUT), dtype=jnp.float32) * s, 'b2': jnp.zeros((D_OUT,), jnp.float32)}
    _L1_gnn_all = _L1_gnn_setup()
    _L1_gnn_in = {k: v for k, v in _L1_gnn_all.items() if k in ('Wp1', 'bp1', 'Ws1', 'Wn1', 'b1', 'Wp2', 'bp2', 'Ws2', 'Wn2', 'b2')}
    del _L1_gnn_all
    return {'x': x, 'src': src, 'dst': dst, 'edge_attr_17': edge_attr_17, 'L0_gnn_W1': _L0_gnn_in['W1'], 'L0_gnn_b1': _L0_gnn_in['b1'], 'L0_gnn_W2': _L0_gnn_in['W2'], 'L0_gnn_b2': _L0_gnn_in['b2'], 'L0_gnn_Ws': _L0_gnn_in['Ws'], 'L0_gnn_bs': _L0_gnn_in['bs'], 'L0_gnn_Wn': _L0_gnn_in['Wn'], 'L0_gnn_bn': _L0_gnn_in['bn'], 'L1_gnn_Wp1': _L1_gnn_in['Wp1'], 'L1_gnn_bp1': _L1_gnn_in['bp1'], 'L1_gnn_Ws1': _L1_gnn_in['Ws1'], 'L1_gnn_Wn1': _L1_gnn_in['Wn1'], 'L1_gnn_b1': _L1_gnn_in['b1'], 'L1_gnn_Wp2': _L1_gnn_in['Wp2'], 'L1_gnn_bp2': _L1_gnn_in['bp2'], 'L1_gnn_Ws2': _L1_gnn_in['Ws2'], 'L1_gnn_Wn2': _L1_gnn_in['Wn2'], 'L1_gnn_b2': _L1_gnn_in['b2']}

def reference(x, src, dst, edge_attr_17, L0_gnn_W1, L0_gnn_b1, L0_gnn_W2, L0_gnn_b2, L0_gnn_Ws, L0_gnn_bs, L0_gnn_Wn, L0_gnn_bn, L1_gnn_Wp1, L1_gnn_bp1, L1_gnn_Ws1, L1_gnn_Wn1, L1_gnn_b1, L1_gnn_Wp2, L1_gnn_bp2, L1_gnn_Ws2, L1_gnn_Wn2, L1_gnn_b2):
    import jax
    import jax.numpy as jnp

    def _L0_gnn_ref(x, edge_index, edge_attr, W1, b1, W2, b2, Ws, bs, Wn, bn):
        import jax, jax.numpy as jnp
        import numpy as np
        N = 6250
        E = 100000
        D = 96
        ED = 17
        src, dst = (edge_index[0], edge_index[1])
        h = jax.nn.relu(edge_attr @ W1.T + b1)
        w = h @ W2.T + b2
        msg = w * x[src]
        agg = jax.ops.segment_sum(msg, dst, num_segments=x.shape[0])
        return jax.nn.relu(x @ Ws.T + bs + agg @ Wn.T + bn)

    def _L1_gnn_ref(x, src, dst, Wp1, bp1, Ws1, Wn1, b1, Wp2, bp2, Ws2, Wn2, b2):
        import jax, jax.numpy as jnp
        import numpy as np
        N_NODES = 6250
        N_EDGES = 100000
        D_IN = 96
        D_HID = 96
        D_OUT = 96
        EPS = 1e-12

        def _sage_pool_layer(x, src, dst, Wp, bp, Ws, Wn, b, n_nodes):
            m = jax.nn.relu(x @ Wp + bp)
            msgs = m[src]
            agg = jax.ops.segment_max(msgs, dst, num_segments=n_nodes)
            agg = jnp.where(jnp.isfinite(agg), agg, 0.0)
            return x @ Ws + agg @ Wn + b

        def _l2norm(h):
            n = jnp.linalg.norm(h, axis=1, keepdims=True)
            return h / jnp.maximum(n, EPS)
        n = x.shape[0]
        h = _sage_pool_layer(x, src, dst, Wp1, bp1, Ws1, Wn1, b1, n)
        h = jax.nn.relu(h)
        h = _l2norm(h)
        h = _sage_pool_layer(h, src, dst, Wp2, bp2, Ws2, Wn2, b2, n)
        h = _l2norm(h)
        return h
    edge_index = jnp.stack([src, dst])
    x = _layernorm(x + _L0_gnn_ref(x, edge_index, edge_attr_17, L0_gnn_W1, L0_gnn_b1, L0_gnn_W2, L0_gnn_b2, L0_gnn_Ws, L0_gnn_bs, L0_gnn_Wn, L0_gnn_bn), axis=-1)
    x = _layernorm(x + _L1_gnn_ref(x, src, dst, L1_gnn_Wp1, L1_gnn_bp1, L1_gnn_Ws1, L1_gnn_Wn1, L1_gnn_b1, L1_gnn_Wp2, L1_gnn_bp2, L1_gnn_Ws2, L1_gnn_Wn2, L1_gnn_b2), axis=-1)
    return x

_drawn_inputs = setup_inputs


def setup_inputs(seed=0):
    import zlib

    import numpy as np

    out = dict(_drawn_inputs(seed))
    spreads = {'L1_gnn_bp1': (0.0, 0.1),
     'L1_gnn_b1': (0.0, 0.1),
     'L1_gnn_bp2': (0.0, 0.1),
     'L1_gnn_b2': (0.0, 0.1)}
    factors = {}
    for name, (base, spread) in spreads.items():
        noise = np.random.default_rng([zlib.crc32(name.encode()), seed]).standard_normal(out[name].shape)
        drawn = base * np.exp(spread * noise) if base else spread * noise
        out[name] = jnp.asarray(drawn.astype(out[name].dtype))
    for name, factor in factors.items():
        out[name] = (out[name] * factor).astype(out[name].dtype)
    return out
```

```python
from contextlib import ExitStack

import numpy as np

import concourse.bass as bass
from concourse import mybir

ALU = mybir.AluOpType
ACT = mybir.ActivationFunctionType
AX = mybir.AxisListType
F32 = mybir.dt.float32
BF16 = mybir.dt.bfloat16
I32 = mybir.dt.int32

P = 128
N, E, D, ED = 12500, 200000, 96, 17

G = 28
NB = 56
T = G * NB
EP = P * T
assert EP >= E and (P - 1) * T < E
GQ = 4
NG = G // GQ
assert NG * ED <= P

NBLK = -(-N // P)
NP = NBLK * P
C = 7
NC = NBLK // C
assert NC * C == NBLK and NC % 2 == 0
ZROW = EP
D1 = D + 1

LN_EPS = 1e-5
L2_EPS = 1e-12


def build(nc, src, dst, ea, x_rows, x_pm, xT, w1z, b1, w2a, wsa, wn, wpsa, out):
    with ExitStack() as ctx:
        def sb(name, shape, dt=F32):
            return ctx.enter_context(nc.sbuf_tensor(name, shape, dt))

        def sem(name):
            return ctx.enter_context(nc.semaphore(name))

        def sem2(name):
            return [sem(f"{name}{s}") for s in range(2)]

        states = nc.dram_tensor("states", (EP + 1, D), F32).ap()
        states_v = states[0:EP, :].rearrange("(p b g) d -> p b (g d)", p=P, b=NB)
        m_tab = [nc.dram_tensor(f"m_tab{i}", (NP, D), F32).ap() for i in range(2)]
        m_tab_v = [m.rearrange("(k p) d -> p k d", p=P) for m in m_tab]
        self_tab = [nc.dram_tensor(f"self_tab{i}", (P, NBLK * D), F32).ap() for i in range(3)]
        x1_tab = nc.dram_tensor("x1_tab", (P, NBLK * D), F32).ap()

        src_idx = sb("src_idx", [P, 2, G], I32)
        ring = sb("ring", [P, 2, G, D])
        run = sb("run", [P, 2, G, D])
        dst_i = sb("dst_i", [P, T], I32)
        dst_hi_i = sb("dst_hi_i", [P, T], I32)
        dst_lo_i = sb("dst_lo_i", [P, T], I32)
        dst_hi = sb("dst_hi", [P, T], BF16)
        dst_lo = sb("dst_lo", [P, T], BF16)
        keep = sb("keep", [P, T])
        keep_b = sb("keep_b", [P, 2, G])
        zeros_w = sb("zeros_w", [P, P], BF16)
        iota_i = sb("iota_i", [P, P], I32)
        iota = sb("iota", [P, P], BF16)
        hot_hi = sb("hot_hi", [P, G, NBLK], BF16)
        hot_lo = sb("hot_lo", [P, G, P], BF16)
        ea_sb = sb("ea_sb", [NG * ED, 2, GQ * P])
        hT = sb("hT", [D1, 2, GQ * P])
        w1z_sb = sb("w1z_sb", [NG * ED, NG, D])
        b1_sb = sb("b1_sb", [D, 1])
        w2a_sb = sb("w2a_sb", [D1, D])
        ident = sb("ident", [P, P])
        upper = sb("upper", [P, P])
        ones = sb("ones", [P, P])
        ends_f = sb("ends_f", [P, 2])
        ends_b = sb("ends_b", [P, 2, D])
        last_row = sb("last_row", [D, P])
        whole_row = sb("whole_row", [D, P])
        cont_row = sb("cont_row", [D, P])
        pass_row = sb("pass_row", [D, P])
        same_first = sb("same_first", [P, T])
        head_n = sb("head_n", [P, 1])
        head_base_i = sb("head_base_i", [P, 1], I32)
        head_base = sb("head_base", [P, 1])
        head_idx = sb("head_idx", [P, 1], I32)
        carry = sb("carry", [D, P + 1])
        carry_in = sb("carry_in", [D, P])
        head_rows = sb("head_rows", [P, D])
        head_fixed = sb("head_fixed", [P, D])
        hist = sb("hist", [P, NBLK])
        nodes_cum = sb("nodes_cum", [P, NBLK])
        end_a = sb("end_a", [P, NBLK])
        end_b = sb("end_b", [P, NBLK])
        some = sb("some", [P, NBLK])
        end_idx = sb("end_idx", [P, NBLK + 2 * C], I32)
        end_slot = sb("end_slot", [P, 2, C], I32)
        agg = sb("agg", [P, 2, C, D])
        aggT = sb("aggT", [D, 2, C * P])
        self_in = sb("self_in", [P, 2, C, D])
        res_in = sb("res_in", [P, 2, C, D])
        t1 = sb("t1", [P, C, D])
        t2 = sb("t2", [P, C, D])
        sq = sb("sq", [P, C, D])
        stat = sb("stat", [P, 8, C])
        node_new = sb("node_new", [P, 2, C, D])
        nodeT = sb("nodeT", [D + 2, 2, C * P])
        m_sb = sb("m_sb", [P, 2, C, D])
        self_out = sb("self_out", [P, 2, C, D])
        wsa_sb = sb("wsa_sb", [D + 2, D])
        wn_sb = sb("wn_sb", [D, 3, D])
        wpsa_sb = sb("wpsa_sb", [D1, 2, 2 * D])
        eps_col = sb("eps_col", [P, 1])
        zero_col = sb("zero_col", [P, 1])
        zrow = sb("zrow", [1, D])

        ps = [ctx.enter_context(nc.psum_tensor(f"ps{i}", [P, 512], F32)) for i in range(8)]
        ps_h, ps_w, ps_hist = ps[0:2], ps[2:4], ps[4]
        ps_t, ps_o, ps_ms = ps[0:2], ps[2:4], ps[4:8]

        s_credit = sem("s_credit")
        idx_loaded = sem2("idx_loaded")
        dst_loaded, weights_loaded = sem("dst_loaded"), sem("weights_loaded")
        ea_loaded, xT_loaded = sem2("ea_loaded"), sem2("xT_loaded")
        gathered = [sem2(f"gathered{ph}_") for ph in range(3)]
        turn_begun = sem("turn_begun")
        step_done = sem("step_done")
        run_stored = sem2("run_stored")
        h_ready, h_copied, w_ready, msg_done = sem("h_ready"), sem("h_copied"), sem("w_ready"), sem("msg_done")
        hot_ready, hist_added = sem("hot_ready"), sem("hist_added")
        consts_made, prep = sem("consts_made"), sem("prep")
        keep_copied = sem("keep_copied")
        ends_ready, rows_ready = sem("ends_ready"), sem("rows_ready")
        tables_ready = sem("tables_ready")
        last_T, carried, carry_ready, carry_back = sem("last_T"), sem("carried"), sem("carry_ready"), sem("carry_back")
        head_got, head_ready, head_put = sem("head_got"), sem("head_ready"), sem("head_put")
        hist_copied, hist_summed, end_step, end_ready = sem("hist_copied"), sem("hist_summed"), sem("end_step"), sem("end_ready")
        agg_gathered = sem2("agg_gathered")
        aggT_ready, aggT_copied = sem("aggT_ready"), sem("aggT_copied")
        o_ready, o_used = sem("o_ready"), sem("o_used")
        node_step, node_ready = sem("node_step"), sem("node_ready")
        sq_in, sq_ready, var_in, std_ready = sem("sq_in"), sem("sq_ready"), sem("var_in"), sem("std_ready")
        nodeT_ready, nodeT_copied = sem("nodeT_ready"), sem("nodeT_copied")
        ms_ready, m_copied, self_copied = sem("ms_ready"), sem("m_copied"), sem("self_copied")
        node_in, m_stored, self_stored, new_stored = sem2("node_in"), sem2("m_stored"), sem2("self_stored"), sem2("new_stored")
        pre_ready, pre_copied = sem("pre_ready"), sem("pre_copied")
        zero_ready, zero_stored = sem("zero_ready"), sem("zero_stored")

        block = ctx.enter_context(nc.Block())

        def in_pairs(eng, n, body, last=None):
            with eng.Fori(0, n // 2 - (last is not None)) as i:
                for s in range(2):
                    body(i, s, i * 2 + s)
            if last is not None:
                for s in range(2):
                    last(n // 2 - 1, s, n - 2 + s)

        def staggered(eng, first, second):
            first(0, 0, 0)
            with eng.Fori(0, NC // 2 - 1) as i:
                first(i, 1, i * 2 + 1)
                second(i, 0, i * 2)
                first(i + 1, 0, i * 2 + 2)
                second(i, 1, i * 2 + 1)
            first(NC // 2 - 1, 1, NC - 1)
            second(NC // 2 - 1, 0, NC - 2)
            second(NC // 2 - 1, 1, NC - 1)

        def flat(ap):
            return ap.rearrange("p c d -> p (c d)")

        @block.sync
        def _(sp):
            sp.sem_inc(step_done, 2 * G + 1)
            sp.sem_inc(h_copied, 2)
            sp.sem_inc(w_ready, 2)
            sp.sem_inc(msg_done, 2)
            sp.sem_inc(hist_added, 1)
            sp.sem_inc(pre_copied, 1)
            sp.sem_inc(nodeT_copied, 2)
            sp.sem_inc(aggT_copied, 2)
            sp.sem_inc(o_used, 1)
            sp.sem_inc(m_copied, 1)
            sp.sem_inc(self_copied, 1)
            for s in range(2):
                sp.sem_inc(run_stored[s], 16)
                sp.sem_inc(m_stored[s], 16)
                sp.sem_inc(self_stored[s], 16)
                sp.sem_inc(new_stored[s], 16)
            for s in range(2):
                sp.dma_start(src_idx[:, s, :], src[:, s * G:(s + 1) * G]).then_inc(idx_loaded[s], 16)
            sp.dma_start(dst_i[:, :], dst).then_inc(dst_loaded, 16)
            for s in range(2):
                sp.dma_start(nodeT[0:D, s, :], xT[:, s * C * P:(s + 1) * C * P]).then_inc(xT_loaded[s], 16)
            weights = [(wsa_sb[:, :], wsa), (w1z_sb[:, :, :], w1z), (b1_sb[:, :], b1), (w2a_sb[:, :], w2a),
                       (wn_sb[:, :, :], wn), (wpsa_sb[:, :, :], wpsa)]
            for to, of in weights:
                sp.dma_start(to, of).then_inc(weights_loaded, 16)
            for s in range(2):
                sp.dma_start(ea_sb[:, s, :], ea[:, s, :]).then_inc(ea_loaded[s], 16)
            sp.wait_ge(zero_ready, 1)
            sp.dma_start(states[ZROW:ZROW + 1, :], zrow[:, :]).then_inc(zero_stored, 16)

            def pre(i, s, j, load=True):
                sp.wait_ge(pre_copied, j + 2)
                if load:
                    sp.dma_start(nodeT[0:D, s, :], xT[:, bass.ds((j + 2) * (C * P), C * P)]).then_inc(xT_loaded[s], 16)
                sp.dma_start(self_tab[0][:, bass.ds(j * (C * D), C * D)], flat(self_out[:, s])).then_inc(self_stored[s], 16)

            in_pairs(sp, NC, pre, lambda i, s, j: pre(i, s, j, False))

            for ph in range(3):
                def edge(i, s, b, load=True):
                    if load:
                        sp.wait_ge(gathered[ph][s], i * (16 * G) + 16 * G)
                        sp.dma_start(src_idx[:, s, :], src[:, bass.ds((b + 2) * G, G)]).then_inc(idx_loaded[s], 16)
                    sp.wait_ge(step_done, b * G + (ph * T + 3 * G + 1))
                    if load and ph == 0:
                        sp.wait_ge(w_ready, b * NG + NG + 2)
                        sp.dma_start(ea_sb[:, s, :], ea[:, bass.ds(b + 2, 1), :].rearrange("a b c -> a (b c)")).then_inc(ea_loaded[s], 16)
                    sp.dma_start(states_v[:, bass.ds(b, 1), :].rearrange("p b c -> p (b c)"), flat(run[:, s])).then_inc(run_stored[s], 16)

                in_pairs(sp, NB, edge, lambda i, s, b: edge(i, s, b, False))
                if ph < 2:
                    for s in range(2):
                        sp.wait_ge(gathered[ph][s], 16 * G * NB // 2)
                        sp.dma_start(src_idx[:, s, :], src[:, s * G:(s + 1) * G]).then_inc(idx_loaded[s], 16)

                def load_nodes(s, j):
                    sp.dma_start(flat(self_in[:, s]), self_tab[ph][:, bass.ds(j * (C * D), C * D)]).then_inc(node_in[s], 16)
                    if ph != 1:
                        x_in = x_pm if ph == 0 else x1_tab
                        sp.dma_start(flat(res_in[:, s]), x_in[:, bass.ds(j * (C * D), C * D)]).then_inc(node_in[s], 16)

                def node(i, s, j, load=True):
                    sp.wait_ge(node_ready, j + (ph * NC + 1))
                    if load:
                        load_nodes(s, j + 2)
                    if ph != 1:
                        x_out = x1_tab if ph == 0 else out
                        sp.dma_start(x_out[:, bass.ds(j * (C * D), C * D)], flat(node_new[:, s])).then_inc(new_stored[s], 16)
                    if ph < 2:
                        sp.wait_ge(m_copied, j + (ph * NC + 2))
                        sp.dma_start(m_tab_v[ph][:, bass.ds(j * C, C), :], m_sb[:, s]).then_inc(m_stored[s], 16)
                        sp.wait_ge(self_copied, j + (ph * NC + 2))
                        sp.dma_start(self_tab[ph + 1][:, bass.ds(j * (C * D), C * D)], flat(self_out[:, s])).then_inc(self_stored[s], 16)

                half = 16 * (NC // 2)
                for s in range(2):
                    sp.wait_ge(self_stored[s], half * (ph + 1) + 16)
                    if ph == 2:
                        sp.wait_ge(new_stored[s], half + 16)
                for s in range(2):
                    load_nodes(s, s)
                in_pairs(sp, NC, node, lambda i, s, j: node(i, s, j, False))
            for s in range(2):
                sp.wait_ge(new_stored[s], half * 2 + 16)

        @block.gpsimd
        def _(pool):
            pool.memset(ones[:, :], 1.0).then_inc(prep, 1)
            pool.iota(iota_i[:, :], [[1, P]], base=0, channel_multiplier=0)
            pool.iota(head_base_i[:, :], [[1, 1]], base=-1, channel_multiplier=T)
            pool.wait_ge(prep, 1)
            pool.affine_select(out=ident[:, :], in_=ones[:, :], compare_op=ALU.is_equal, fill=0.0, base=0,
                               pattern=[[-1, P]], channel_multiplier=1)
            pool.affine_select(out=upper[:, :], in_=ones[:, :], compare_op=ALU.is_ge, fill=0.0, base=0,
                               pattern=[[1, P]], channel_multiplier=-1).then_inc(consts_made, 1)

            for ph in range(3):
                table = x_rows if ph == 0 else m_tab[ph - 1]
                if ph:
                    for s in range(2):
                        pool.wait_ge(m_stored[s], 16 * (NC // 2) * ph + 16)

                def gather(i, s, b):
                    pool.wait_ge(idx_loaded[s], i * 16 + (ph * 16 * (NB // 2) + 16))
                    pool.wait_ge(step_done, b * G + (ph * T + G + 1))
                    pool.sem_inc(turn_begun, 1)
                    for g in range(G):
                        pool.indirect_dma_start(ring[:, s, g, :], None, table,
                                                bass.IndirectOffsetOnAxis(src_idx[:, s, g:g + 1], 0)
                                                ).then_inc(gathered[ph][s], 16)

                in_pairs(pool, NB, gather)

                for s in range(2):
                    pool.wait_ge(run_stored[s], 16 * (NB // 2) * (ph + 1) + 16)
                pool.wait_ge(tables_ready, 1)
                pool.wait_ge(zero_stored, 16)
                pool.indirect_dma_start(head_rows[:, :], None, states,
                                        bass.IndirectOffsetOnAxis(head_idx[:, 0:1], 0)).then_inc(head_got, 16)
                pool.wait_ge(head_ready, ph + 1)
                pool.indirect_dma_start(states, bass.IndirectOffsetOnAxis(head_idx[:, 0:1], 0),
                                        head_fixed[:, :], None).then_inc(head_put, 16)
                pool.wait_ge(head_put, 16 * (ph + 1))

                def node_gather(i, s, j):
                    pool.wait_ge(end_ready, j + (ph * (NC + 2) + 1))
                    pool.wait_ge(aggT_copied, j + (ph * NC + 1))
                    pool.sem_inc(turn_begun, 1)
                    for c in range(C):
                        pool.indirect_dma_start(agg[:, s, c, :], None, states,
                                                bass.IndirectOffsetOnAxis(end_slot[:, s, c:c + 1], 0)
                                                ).then_inc(agg_gathered[s], 16)

                in_pairs(pool, NC, node_gather)

        @block.tensor
        def _(pe):
            pe.wait_ge(weights_loaded, 16 * 6)

            def pre(i, s, j):
                pe.wait_ge(xT_loaded[s], i * 16 + 16)
                pe.wait_ge(pre_copied, j + 1)
                for c in range(C):
                    mm = nc.tensor.matmul(ps_o[c // 4][:, (c % 4) * D:(c % 4 + 1) * D],
                                          nodeT[:, s, c * P:(c + 1) * P], wsa_sb[:, :], start=True, stop=True)
                mm.then_inc(pre_ready, 1)

            pe.wait_ge(tables_ready, 2)
            in_pairs(pe, NC, pre)

            pe.wait_ge(consts_made, 1)
            pe.wait_ge(ends_ready, 1)
            for n in range(2):
                mm = nc.tensor.matmul(ps_ms[1][0:D, n * P:(n + 1) * P], ends_b[:, n, :], ident[:, :], start=True, stop=True)
            mm.then_inc(rows_ready, 1)

            def hidden(i, s, b, g):
                bank = (s * NG + g) % 2
                pe.wait_ge(h_copied, b * NG + (g + 1))
                nc.tensor.matmul(ps_h[bank][0:D, :], w1z_sb[:, g, :], ea_sb[:, s, :], start=True, stop=True
                                 ).then_inc(h_ready, 1)

            def weight(i, s, b, g):
                bank = (s * NG + g) % 2
                pe.wait_ge(h_copied, b * NG + (g + 3))
                pe.wait_ge(msg_done, b * NG + (g + 1))
                for q in range(GQ):
                    mm = nc.tensor.matmul(ps_w[bank][:, q * D:(q + 1) * D], hT[:, bank, q * P:(q + 1) * P],
                                          w2a_sb[:, :], start=True, stop=True)
                mm.then_inc(w_ready, 1)

            def edge(i, s, b):
                pe.wait_ge(ea_loaded[s], i * 16 + 16)
                hidden(i, s, b, 0)
                for g in range(1, NG):
                    hidden(i, s, b, g)
                    weight(i, s, b, g - 1)
                weight(i, s, b, NG - 1)
                pe.wait_ge(hot_ready, b + 1)
                for g in range(G):
                    mm = nc.tensor.matmul(ps_hist[:, 0:NBLK], hot_lo[:, g, :], hot_hi[:, g, :],
                                          start=False, stop=False, skip_group_check=True)
                mm.then_inc(hist_added, 1)

            nc.tensor.matmul(ps_hist[:, 0:NBLK], zeros_w[:, :], zeros_w[:, 0:NBLK], start=True, stop=False, skip_group_check=True)
            in_pairs(pe, NB, edge)

            pe.wait_ge(hist_copied, 1)
            nc.tensor.matmul(ps_ms[1][:, 0:NBLK], upper[:, :], hist[:, :], start=True, stop=True)
            nc.tensor.matmul(ps_ms[1][:, P:P + NBLK], ones[:, :], hist[:, :], start=True, stop=True).then_inc(hist_summed, 1)

            for ph in range(3):
                pe.wait_ge(step_done, (ph + 1) * T + 2 * G + 1)
                pe.transpose(ps_t[0][0:D, 0:P], run[:, 1, G - 1, :], ident[:, :]).then_inc(last_T, 1)
                pe.wait_ge(carry_ready, ph + 1)
                pe.transpose(ps_t[1][:, 0:D], carry_in[:, :], ident[0:D, 0:D]).then_inc(carry_back, 1)
                pe.wait_ge(head_ready, ph + 1)

                def first(i, s, j):
                    pe.wait_ge(agg_gathered[s], i * (16 * C) + (ph * 16 * C * (NC // 2) + 16 * C))
                    if ph < 2:
                        pe.wait_ge(nodeT_copied, j + (ph * NC + 1))
                    for c in range(C):
                        mm = pe.transpose(ps_t[c // 4][0:D, (c % 4) * P:(c % 4 + 1) * P], agg[:, s, c, :], ident[:, :])
                    mm.then_inc(aggT_ready, 1)
                    pe.wait_ge(aggT_copied, j + (ph * NC + 3))
                    pe.wait_ge(o_used, j + (ph * NC + 1))
                    for c in range(C):
                        mm = nc.tensor.matmul(ps_o[c // 4][:, (c % 4) * D:(c % 4 + 1) * D], aggT[:, s, c * P:(c + 1) * P],
                                              wn_sb[:, ph, :], start=True, stop=True)
                    mm.then_inc(o_ready, 1)

                def second(i, s, j):
                    pe.wait_ge(node_ready, j + (ph * NC + 1))
                    for c in range(C):
                        mm = pe.transpose(ps_t[c // 4][0:D, (c % 4) * P:(c % 4 + 1) * P], node_new[:, s, c, :], ident[:, :])
                    mm.then_inc(nodeT_ready, 1)
                    pe.wait_ge(nodeT_copied, j + (ph * NC + 3))
                    pe.wait_ge(m_copied, j + (ph * NC + 1))
                    pe.wait_ge(self_copied, j + (ph * NC + 1))
                    for c in range(C):
                        mm = nc.tensor.matmul(ps_ms[c // 2][:, (c % 2) * 2 * D:(c % 2 + 1) * 2 * D],
                                              nodeT[0:D1, s, c * P:(c + 1) * P], wpsa_sb[:, ph, :], start=True, stop=True)
                    mm.then_inc(ms_ready, 1)

                if ph < 2:
                    staggered(pe, first, second)
                else:
                    in_pairs(pe, NC, first)

        @block.scalar
        def _(act):
            act.wait_ge(weights_loaded, 16 * 6)
            act.wait_ge(tables_ready, 2)

            def edge(i, s, b):
                for g in range(NG):
                    bank = (s * NG + g) % 2
                    act.wait_ge(h_ready, b * NG + (g + 1))
                    act.wait_ge(w_ready, b * NG + (g + 1))
                    nc.scalar.activation(hT[0:D, bank, :], ps_h[bank][0:D, :], ACT.Relu, bias=b1_sb[:, 0:1]
                                         ).then_inc(h_copied, 1)

            in_pairs(act, NB, edge)

            for ph in range(3):
                def square(j):
                    act.wait_ge(sq_in, j)
                    nc.scalar.activation(flat(sq[:, :, :]), flat(t2[:, :, :]), ACT.Square, bias=zero_col[:, 0:1]).then_inc(sq_ready, 1)

                def root(j, eps):
                    act.wait_ge(var_in, j)
                    nc.scalar.activation(stat[:, 3, :], stat[:, 2, :], ACT.Sqrt, bias=eps[:, 0:1]).then_inc(std_ready, 1)

                def first(i, s, j):
                    act.wait_ge(aggT_ready, j + (ph * NC + 1))
                    nc.scalar.activation(aggT[:, s, 0:4 * P], ps_t[0][0:D, :], ACT.Copy)
                    nc.scalar.activation(aggT[:, s, 4 * P:C * P], ps_t[1][0:D, 0:(C - 4) * P], ACT.Copy).then_inc(aggT_copied, 1)
                    if ph == 0:
                        square(j + 1)
                        root(j + 1, eps_col)
                    elif ph == 1:
                        square(j + (NC + 1))
                        root(j + (NC + 1), zero_col)
                    else:
                        square(j * 2 + (2 * NC + 1))
                        root(j * 2 + (2 * NC + 1), zero_col)
                        square(j * 2 + (2 * NC + 2))
                        root(j * 2 + (2 * NC + 2), eps_col)

                def second(i, s, j):
                    act.wait_ge(nodeT_ready, j + (ph * NC + 1))
                    nc.scalar.activation(nodeT[0:D, s, 0:4 * P], ps_t[0][0:D, :], ACT.Copy)
                    nc.scalar.activation(nodeT[0:D, s, 4 * P:C * P], ps_t[1][0:D, 0:(C - 4) * P], ACT.Copy).then_inc(nodeT_copied, 1)
                    act.wait_ge(ms_ready, j + (ph * NC + 1))
                    act.wait_ge(m_stored[s], i * 16 + (ph * 16 * (NC // 2) + 16))
                    ms = [ps_ms[q][:, 0:min(2, C - 2 * q) * 2 * D].rearrange("p (w d) -> p w d", d=2 * D) for q in range(4)]
                    for q in range(4):
                        last = nc.scalar.activation(m_sb[:, s, 2 * q:min(2 * q + 2, C), :], ms[q][:, :, 0:D],
                                                    ACT.Relu, bias=zero_col[:, 0:1])
                    last.then_inc(m_copied, 1)
                    act.wait_ge(self_stored[s], i * 16 + ((ph + 1) * 16 * (NC // 2) + 16))
                    for q in range(4):
                        last = nc.scalar.activation(self_out[:, s, 2 * q:min(2 * q + 2, C), :], ms[q][:, :, D:2 * D], ACT.Copy)
                    last.then_inc(self_copied, 1)

                if ph < 2:
                    staggered(act, first, second)
                else:
                    in_pairs(act, NC, first)

        @block.vector
        def _(dve):
            done = [0]

            def chain(ins):
                done[0] += 1
                ins.then_inc(end_step, 1)
                dve.wait_ge(end_step, done[0])

            v = nc.vector
            chain(v.memset(run[:, 1, G - 1, :], 0.0))
            v.memset(zrow[:, :], 0.0).then_inc(zero_ready, 1)
            v.memset(zeros_w[:, :], 0.0)
            v.memset(eps_col[:, :], LN_EPS)
            v.memset(zero_col[:, :], 0.0)
            v.memset(nodeT[D:D + 2, :, :], 1.0)
            v.memset(carry[:, 0:1], 0.0)
            v.memset(cont_row[:, 0:1], 0.0)
            v.memset(keep[:, 0:1], 0.0)
            v.memset(end_idx[:, NBLK:], 0)
            v.memset(hT[D:D1, :, :], 1.0)
            v.memset(head_rows[:, 0:1], 0.0).then_inc(tables_ready, 2)

            def pre(i, s, j):
                dve.wait_ge(pre_ready, j + 1)
                dve.wait_ge(self_stored[s], i * 16 + 16)
                v.tensor_copy(flat(self_out[:, s, 0:4]), ps_o[0][:, 0:4 * D])
                v.tensor_copy(flat(self_out[:, s, 4:C]), ps_o[1][:, 0:(C - 4) * D]).then_inc(pre_copied, 1)

            in_pairs(dve, NC, pre)

            dve.wait_ge(dst_loaded, 16)
            dve.wait_ge(consts_made, 1)
            v.tensor_copy(ends_f[:, 0:1], dst_i[:, 0:1])
            chain(v.tensor_copy(ends_f[:, 1:2], dst_i[:, T - 1:T]))
            v.tensor_scalar(ends_b[:, 0, :], ones[:, 0:D], ends_f[:, 0:1], None, ALU.mult)
            v.tensor_scalar(ends_b[:, 1, :], ones[:, 0:D], ends_f[:, 1:2], None, ALU.mult).then_inc(ends_ready, 1)
            v.tensor_tensor(keep[:, 1:T], dst_i[:, 1:T], dst_i[:, 0:T - 1], ALU.is_equal)
            v.tensor_scalar(dst_hi_i[:, :], dst_i[:, :], 7, None, ALU.arith_shift_right)
            chain(v.tensor_scalar(dst_lo_i[:, :], dst_i[:, :], P - 1, None, ALU.bitwise_and))
            v.tensor_copy(dst_hi[:, :], dst_hi_i[:, :])
            v.tensor_copy(dst_lo[:, :], dst_lo_i[:, :])
            v.tensor_copy(head_base[:, :], head_base_i[:, :])
            v.tensor_copy(iota[:, :], iota_i[:, :])
            chain(v.tensor_scalar(same_first[:, :], dst_i[:, :], ends_f[:, 0:1], None, ALU.is_equal))
            chain(v.tensor_reduce(head_n[:, :], same_first[:, :], AX.X, ALU.add))
            v.tensor_tensor(head_idx[:, :], head_n[:, :], head_base[:, :], ALU.add)
            dve.wait_ge(rows_ready, 1)
            chain(v.tensor_copy(last_row[:, :], ps_ms[1][0:D, P:2 * P]))
            v.tensor_tensor(cont_row[:, 1:P], ps_ms[1][0:D, 1:P], last_row[:, 0:P - 1], ALU.is_equal)
            chain(v.tensor_tensor(whole_row[:, :], ps_ms[1][0:D, 0:P], last_row[:, :], ALU.is_equal))
            chain(v.tensor_tensor(pass_row[:, :], whole_row[:, :], cont_row[:, :], ALU.mult))

            for ph in range(3):
                merge = ALU.add if ph == 0 else ALU.max

                def edge(i, s, b):
                    dve.wait_ge(step_done, b * G + (ph * T + G + 1))
                    v.tensor_scalar(keep_b[:, s, :], keep[:, bass.ds(b * G, G)], 0.0, None, ALU.add).then_inc(keep_copied, 1)
                    if ph == 0:
                        dve.wait_ge(hist_added, b + 1)
                        v.tensor_tensor(hot_hi[:, :, :], iota[:, 0:NBLK].unsqueeze(1).to_broadcast([P, G, NBLK]),
                                        dst_hi[:, bass.ds(b * G, G)].unsqueeze(2).to_broadcast([P, G, NBLK]), ALU.is_equal)
                        v.tensor_tensor(hot_lo[:, :, :], iota[:, :].unsqueeze(1).to_broadcast([P, G, P]),
                                        dst_lo[:, bass.ds(b * G, G)].unsqueeze(2).to_broadcast([P, G, P]), ALU.is_equal
                                        ).then_inc(hot_ready, 1)
                    dve.wait_ge(keep_copied, b + (ph * NB + 1))
                    dve.wait_ge(gathered[ph][s], i * (16 * G) + 16 * G)
                    dve.wait_ge(run_stored[s], i * 16 + (ph * 16 * (NB // 2) + 16))
                    for g in range(G):
                        if ph == 0 and g % GQ == 0:
                            n = g // GQ
                            dve.wait_ge(w_ready, b * NG + (n + 3))
                            v.tensor_tensor(flat(ring[:, s, g:g + GQ]), ps_w[(s * NG + n) % 2][:, 0:GQ * D],
                                            flat(ring[:, s, g:g + GQ]), ALU.mult).then_inc(msg_done, 1)
                            dve.wait_ge(msg_done, b * NG + (n + 3))
                        before = run[:, s, g - 1, :] if g else run[:, 1 - s, G - 1, :]
                        dve.wait_ge(step_done, b * G + (ph * T + 2 * G + 1 + g))
                        v.scalar_tensor_tensor(run[:, s, g, :], before, keep_b[:, s, g:g + 1], ring[:, s, g, :],
                                               ALU.mult, merge).then_inc(step_done, 1)

                in_pairs(dve, NB, edge)

                if ph == 0:
                    dve.wait_ge(hist_added, NB + 1)
                    v.tensor_copy(hist[:, :], ps_hist[:, 0:NBLK]).then_inc(hist_copied, 1)
                dve.wait_ge(last_T, ph + 1)
                v.tensor_tensor_scan(carry[:, 1:P + 1], pass_row[:, :], ps_t[0][0:D, 0:P], 0.0, ALU.mult, merge
                                     ).then_inc(carried, 1)
                dve.wait_ge(carried, ph + 1)
                v.tensor_tensor(carry_in[:, :], cont_row[:, :], carry[:, 0:P], ALU.mult).then_inc(carry_ready, 1)
                if ph == 0:
                    dve.wait_ge(hist_summed, 1)
                    chain(v.tensor_tensor_scan(nodes_cum[:, :], ones[:, 0:NBLK], ps_ms[1][:, P:P + NBLK], 0.0, ALU.mult, ALU.add))
                    chain(v.tensor_tensor(end_a[:, :], nodes_cum[:, :], ps_ms[1][:, P:P + NBLK], ALU.subtract))
                    chain(v.tensor_tensor(end_b[:, :], ps_ms[1][:, 0:NBLK], end_a[:, :], ALU.add))
                    v.tensor_scalar(end_a[:, :], end_b[:, :], -float(ZROW + 1), None, ALU.add)
                    chain(v.tensor_scalar(some[:, :], hist[:, :], 0.0, None, ALU.is_gt))
                    chain(v.tensor_tensor(end_b[:, :], end_a[:, :], some[:, :], ALU.mult))
                    chain(v.tensor_scalar(end_idx[:, 0:NBLK], end_b[:, :], float(ZROW), None, ALU.add))
                for s in range(2):
                    v.tensor_copy(end_slot[:, s, :], end_idx[:, s * C:(s + 1) * C]).then_inc(end_ready, 1)
                dve.wait_ge(head_got, 16 * (ph + 1))
                dve.wait_ge(carry_back, ph + 1)
                v.tensor_tensor(head_fixed[:, :], ps_t[1][:, 0:D], head_rows[:, :], merge).then_inc(head_ready, 1)

                n_in = 32 if ph != 1 else 16
                base_in = [0, 32 * (NC // 2), 48 * (NC // 2)][ph]
                n_steps = [6, 3, 9][ph]
                base_steps = [0, 6 * NC, 9 * NC][ph]

                def first(i, s, j):
                    at = [0]

                    def link(ins):
                        at[0] += 1
                        ins.then_inc(node_step, 1)
                        dve.wait_ge(node_step, j * n_steps + (base_steps + at[0]))

                    def wide(k):
                        return stat[:, k, :].unsqueeze(2).to_broadcast([P, C, D])

                    def layer_norm(out_ap, n):
                        link(v.tensor_reduce(stat[:, 0, :], t1[:, :, :], AX.X, ALU.add))
                        link(v.tensor_scalar(stat[:, 4, :], stat[:, 0, :], 1.0 / D, None, ALU.mult))
                        v.tensor_tensor(t2[:, :, :], t1[:, :, :], wide(4), ALU.subtract).then_inc(sq_in, 1)
                        dve.wait_ge(sq_ready, n)
                        link(v.tensor_reduce(stat[:, 1, :], sq[:, :, :], AX.X, ALU.add))
                        v.tensor_scalar(stat[:, 2, :], stat[:, 1, :], 1.0 / D, None, ALU.mult).then_inc(var_in, 1)
                        dve.wait_ge(std_ready, n)
                        link(v.reciprocal(stat[:, 5, :], stat[:, 3, :]))
                        v.tensor_tensor(out_ap, t2[:, :, :], wide(5), ALU.mult).then_inc(node_ready, 1)

                    def l2_scale(n):
                        dve.wait_ge(sq_ready, n)
                        v.tensor_reduce(stat[:, 2, :], sq[:, :, :], AX.X, ALU.add).then_inc(var_in, 1)
                        dve.wait_ge(std_ready, n)
                        link(v.tensor_scalar(stat[:, 4, :], stat[:, 3, :], L2_EPS, None, ALU.max))
                        link(v.reciprocal(stat[:, 5, :], stat[:, 4, :]))

                    dve.wait_ge(o_ready, j + (ph * NC + 1))
                    v.tensor_scalar(end_slot[:, s, :], end_idx[:, bass.ds((j + 2) * C, C)], 0, None, ALU.add).then_inc(end_ready, 1)
                    dve.wait_ge(node_in[s], i * n_in + (base_in + n_in))
                    v.tensor_tensor(flat(t1[:, 0:4]), ps_o[0][:, 0:4 * D], flat(self_in[:, s, 0:4]), ALU.add)
                    link(v.tensor_tensor(flat(t1[:, 4:C]), ps_o[1][:, 0:(C - 4) * D], flat(self_in[:, s, 4:C]), ALU.add))
                    v.memset(stat[:, 6, 0:1], 0.0).then_inc(o_used, 1)
                    if ph == 0:
                        link(v.scalar_tensor_tensor(t1[:, :, :], t1[:, :, :], 0.0, res_in[:, s], ALU.max, ALU.add))
                        dve.wait_ge(new_stored[s], i * 16 + 16)
                        layer_norm(node_new[:, s], j + 1)
                    elif ph == 1:
                        v.tensor_scalar(t2[:, :, :], t1[:, :, :], 0.0, None, ALU.max).then_inc(sq_in, 1)
                        l2_scale(j + (NC + 1))
                        v.tensor_tensor(node_new[:, s], t2[:, :, :], wide(5), ALU.mult).then_inc(node_ready, 1)
                    else:
                        v.tensor_copy(t2[:, :, :], t1[:, :, :]).then_inc(sq_in, 1)
                        l2_scale(j * 2 + (2 * NC + 1))
                        link(v.tensor_tensor(t1[:, :, :], t2[:, :, :], wide(5), ALU.mult))
                        link(v.tensor_tensor(t1[:, :, :], t1[:, :, :], res_in[:, s], ALU.add))
                        dve.wait_ge(new_stored[s], i * 16 + (16 * (NC // 2) + 16))
                        layer_norm(node_new[:, s], j * 2 + (2 * NC + 2))
                    assert at[0] == n_steps

                in_pairs(dve, NC, first)


def kernel(**inputs):
    from concourse import bacc
    from concourse.bass_utils import run_bass_kernel_spmd

    a = {k: np.asarray(v) for k, v in inputs.items()}
    f32, i32 = np.float32, np.int32

    def rows(x, n, fill=0):
        pad = np.full((n - x.shape[0],) + x.shape[1:], fill, x.dtype)
        return np.concatenate([x, pad])

    src = rows(a["src"], EP).reshape(P, T)
    dst = rows(a["dst"], EP, NP).reshape(P, T)
    ea = rows(a["edge_attr_17"], EP).reshape(P, NB, NG, GQ, ED).transpose(2, 4, 1, 3, 0).reshape(NG * ED, NB, GQ * P)
    x = rows(a["x"], NP)
    x_pm = x.reshape(NBLK, P, D).transpose(1, 0, 2).reshape(P, NBLK * D)
    w1z = np.zeros((NG * ED, NG, D), f32)
    for g in range(NG):
        w1z[g * ED:(g + 1) * ED, g] = a["L0_gnn_W1"].T
    w2a = np.concatenate([a["L0_gnn_W2"].T, a["L0_gnn_b2"][None]])
    wsa = np.concatenate([a["L0_gnn_Ws"].T, a["L0_gnn_bs"][None], a["L0_gnn_bn"][None]])
    wn = np.stack([a["L0_gnn_Wn"].T, a["L1_gnn_Wn1"], a["L1_gnn_Wn2"]], 1)
    wpsa = np.stack([np.concatenate([np.concatenate([a[f"L1_gnn_Wp{n}"], a[f"L1_gnn_bp{n}"][None]]),
                                     np.concatenate([a[f"L1_gnn_Ws{n}"], a[f"L1_gnn_b{n}"][None]])], 1) for n in (1, 2)], 1)
    arrays = {"src": src, "dst": dst, "ea": ea, "x_pm": x_pm, "xT": x.T, "w1z": w1z,
              "b1": a["L0_gnn_b1"][:, None], "w2a": w2a, "wsa": wsa, "wn": wn, "wpsa": wpsa, "x_rows": x}
    arrays = {k: np.ascontiguousarray(v) for k, v in arrays.items()}
    nc = bacc.Bacc("TRN2", target_bir_lowering=False, num_devices=1)
    aps = {k: nc.dram_tensor(k, v.shape, mybir.dt.from_np(v.dtype), kind="ExternalInput").ap() for k, v in arrays.items()}
    out = nc.dram_tensor("out", (P, NBLK * D), F32, kind="ExternalOutput").ap()
    build(nc, **aps, out=out)
    r = run_bass_kernel_spmd(nc, [arrays], core_ids=[0])
    got = np.asarray(r.results[0]["out"])
    return got.reshape(P, NBLK, D).transpose(1, 0, 2).reshape(NP, D)[:N]
```

```python
from contextlib import ExitStack

import numpy as np

import concourse.bass as bass
from concourse import mybir

ALU = mybir.AluOpType
ACT = mybir.ActivationFunctionType
AX = mybir.AxisListType
F32 = mybir.dt.float32
BF16 = mybir.dt.bfloat16
I32 = mybir.dt.int32

P = 128
N, E, D, ED = 12500, 200000, 96, 17

G = 28
NB = 56
T = G * NB
EP = P * T
assert EP >= E and (P - 1) * T < E
GQ = 4
NG = G // GQ
assert NG * ED <= P
PARTS = [(0, 16), (16, G)]

NBLK = -(-N // P)
NP = NBLK * P
C = 7
NC = NBLK // C
assert NC * C == NBLK and NC % 2 == 0
ZROW = EP
TURNS = NB // 2
CS = 4
assert CS * TURNS >= NBLK
D1 = D + 1

LN_EPS = 1e-5
L2_EPS = 1e-12


def build(nc, src, dst, ea, x_rows, x_pm, xT, w1z, b1, w2a, wsa, wn, wpsa, out):
    with ExitStack() as ctx:
        def sb(name, shape, dt=F32):
            return ctx.enter_context(nc.sbuf_tensor(name, shape, dt))

        def sem(name):
            return ctx.enter_context(nc.semaphore(name))

        def sem2(name):
            return [sem(f"{name}{s}") for s in range(2)]

        states = nc.dram_tensor("states", (EP + 1, D), F32).ap()
        states_v = states[0:EP, :].rearrange("(p b g) d -> p b (g d)", p=P, b=NB)
        m_tab = [nc.dram_tensor(f"m_tab{i}", (NP, D), F32).ap() for i in range(2)]
        m_tab_v = [m.rearrange("(k p) d -> p k d", p=P) for m in m_tab]
        self_tab = [nc.dram_tensor(f"self_tab{i}", (P, (TURNS * CS if i == 0 else NBLK) * D), F32).ap()
                    for i in range(3)]
        x1_tab = nc.dram_tensor("x1_tab", (P, NBLK * D), F32).ap()

        src_idx = sb("src_idx", [P, 2, G], I32)
        ring = sb("ring", [P, 2, G, D])
        run = sb("run", [P, 2, G, D])
        dst_i = sb("dst_i", [P, T], I32)
        dst_hi_i = sb("dst_hi_i", [P, T], I32)
        dst_lo_i = sb("dst_lo_i", [P, T], I32)
        dst_hi = sb("dst_hi", [P, T], BF16)
        dst_lo = sb("dst_lo", [P, T], BF16)
        keep = sb("keep", [P, T])
        keep_b = sb("keep_b", [P, 2, G])
        zeros_w = sb("zeros_w", [P, P], BF16)
        iota_i = sb("iota_i", [P, P], I32)
        iota = sb("iota", [P, P], BF16)
        hot_hi = sb("hot_hi", [P, G, NBLK], BF16)
        hot_lo = sb("hot_lo", [P, G, P], BF16)
        ea_sb = sb("ea_sb", [NG * ED, 2, GQ * P])
        hT = sb("hT", [D1, 2, GQ * P])
        w1z_sb = sb("w1z_sb", [NG * ED, NG, D])
        b1_sb = sb("b1_sb", [D, 1])
        w2a_sb = sb("w2a_sb", [D1, D])
        ident = sb("ident", [P, P])
        upper = sb("upper", [P, P])
        ones = sb("ones", [P, P])
        ends_f = sb("ends_f", [P, 2])
        ends_b = sb("ends_b", [P, 2, D])
        last_row = sb("last_row", [D, P])
        whole_row = sb("whole_row", [D, P])
        cont_row = sb("cont_row", [D, P])
        pass_row = sb("pass_row", [D, P])
        same_first = sb("same_first", [P, T])
        head_n = sb("head_n", [P, 1])
        head_base_i = sb("head_base_i", [P, 1], I32)
        head_base = sb("head_base", [P, 1])
        head_idx = sb("head_idx", [P, 1], I32)
        carry = sb("carry", [D, P + 1])
        carry_in = sb("carry_in", [D, P])
        head_rows = sb("head_rows", [P, D])
        head_fixed = sb("head_fixed", [P, D])
        hist = sb("hist", [P, NBLK])
        nodes_cum = sb("nodes_cum", [P, NBLK])
        end_a = sb("end_a", [P, NBLK])
        end_b = sb("end_b", [P, NBLK])
        some = sb("some", [P, NBLK])
        end_idx = sb("end_idx", [P, NBLK + 2 * C], I32)
        end_slot = sb("end_slot", [P, 2, C], I32)
        agg = sb("agg", [P, 2, C, D])
        aggT = sb("aggT", [D, 2, C * P])
        self_in = sb("self_in", [P, 2, C, D])
        res_in = sb("res_in", [P, 2, C, D])
        t1 = sb("t1", [P, C, D])
        t2 = sb("t2", [P, C, D])
        sq = sb("sq", [P, C, D])
        stat = sb("stat", [P, 3, C])
        bn = sb("bn", [P, C, 6])
        mean_var = sb("mean_var", [P, C, 2])
        scratch = sb("scratch", [P, 2])
        node_new = sb("node_new", [P, 2, C, D])
        nodeT = sb("nodeT", [D1, 2, C * P])
        xT_sb = sb("xT_sb", [D + 2, CS * P])
        pre_sb = sb("pre_sb", [P, CS, D])
        m_sb = sb("m_sb", [P, 2, C, D])
        self_out = sb("self_out", [P, 2, C, D])
        wsa_sb = sb("wsa_sb", [D + 2, D])
        wn_sb = sb("wn_sb", [D, 3, D])
        wpsa_sb = sb("wpsa_sb", [D1, 2, 2 * D])
        eps_col = sb("eps_col", [P, 1])
        zero_col = sb("zero_col", [P, 1])
        zrow = sb("zrow", [1, D])

        ps = [ctx.enter_context(nc.psum_tensor(f"ps{i}", [P, 512], F32)) for i in range(8)]
        ps_h, ps_w, ps_hist, ps_pre = ps[0:2], ps[2:4], ps[4], ps[6]
        ps_t, ps_o, ps_ms = ps[0:2], ps[2:4], ps[4:8]

        s_credit = sem("s_credit")
        idx_loaded = sem2("idx_loaded")
        dst_loaded, weights_loaded = sem("dst_loaded"), sem("weights_loaded")
        ea_loaded, xT_loaded = sem2("ea_loaded"), sem("xT_loaded")
        gathered = [[sem2(f"gathered{ph}_{s}_") for s in range(2)] for ph in range(3)]
        turn_begun = sem("turn_begun")
        step_done = sem("step_done")
        run_stored = [sem2(f"run_stored{s}_") for s in range(2)]
        h_ready, h_copied, w_ready, msg_done = sem("h_ready"), sem("h_copied"), sem("w_ready"), sem("msg_done")
        hot_ready, hist_added = sem("hot_ready"), sem("hist_added")
        consts_made, prep = sem("consts_made"), sem("prep")
        keep_copied = sem("keep_copied")
        ends_ready, rows_ready = sem("ends_ready"), sem("rows_ready")
        tables_ready = sem("tables_ready")
        last_T, carried, carry_ready, carry_back = sem("last_T"), sem("carried"), sem("carry_ready"), sem("carry_back")
        head_got, head_ready, head_put = sem("head_got"), sem("head_ready"), sem("head_put")
        hist_copied, hist_summed, end_step, end_ready = sem("hist_copied"), sem("hist_summed"), sem("end_step"), sem("end_ready")
        agg_gathered = sem2("agg_gathered")
        aggT_ready, aggT_copied = sem("aggT_ready"), sem("aggT_copied")
        o_ready, o_used = sem("o_ready"), sem("o_used")
        node_step, node_ready = sem("node_step"), sem("node_ready")
        var_in, std_ready = sem("var_in"), sem("std_ready")
        nodeT_ready, nodeT_copied = sem("nodeT_ready"), sem("nodeT_copied")
        ms_ready, m_copied, self_copied = sem("ms_ready"), sem("m_copied"), sem("self_copied")
        node_in, m_stored, self_stored, new_stored = sem2("node_in"), sem2("m_stored"), sem2("self_stored"), sem2("new_stored")
        pre_ready, pre_copied, pre_stored = sem("pre_ready"), sem("pre_copied"), sem("pre_stored")
        zero_ready, zero_stored = sem("zero_ready"), sem("zero_stored")

        block = ctx.enter_context(nc.Block())

        def in_pairs(eng, n, body, last=None):
            with eng.Fori(0, n // 2 - (last is not None)) as i:
                for s in range(2):
                    body(i, s, i * 2 + s)
            if last is not None:
                for s in range(2):
                    last(n // 2 - 1, s, n - 2 + s)

        def flat(ap):
            return ap.rearrange("p c d -> p (c d)")

        @block.sync
        def _(sp):
            sp.sem_inc(step_done, 2 * G + 1)
            sp.sem_inc(h_copied, 2)
            sp.sem_inc(w_ready, 2)
            sp.sem_inc(msg_done, 2)
            sp.sem_inc(hist_added, 1)
            sp.sem_inc(pre_copied, 1)
            sp.sem_inc(pre_stored, 16)
            sp.sem_inc(nodeT_copied, 2)
            sp.sem_inc(aggT_copied, 2)
            sp.sem_inc(o_used, 1)
            sp.sem_inc(m_copied, 1)
            sp.sem_inc(self_copied, 1)
            for s in range(2):
                for h in range(2):
                    sp.sem_inc(run_stored[s][h], 16)
                sp.sem_inc(m_stored[s], 16)
                sp.sem_inc(self_stored[s], 16)
                sp.sem_inc(new_stored[s], 16)
            for s in range(2):
                sp.dma_start(src_idx[:, s, :], src[:, s * G:(s + 1) * G]).then_inc(idx_loaded[s], 16)
            sp.dma_start(dst_i[:, :], dst).then_inc(dst_loaded, 16)
            weights = [(wsa_sb[:, :], wsa), (w1z_sb[:, :, :], w1z), (b1_sb[:, :], b1), (w2a_sb[:, :], w2a),
                       (wn_sb[:, :, :], wn), (wpsa_sb[:, :, :], wpsa)]
            for to, of in weights:
                sp.dma_start(to, of).then_inc(weights_loaded, 16)
            for s in range(2):
                sp.dma_start(ea_sb[:, s, :], ea[:, s, :]).then_inc(ea_loaded[s], 16)
            sp.dma_start(xT_sb[0:D, :], xT[:, 0:CS * P]).then_inc(xT_loaded, 16)
            sp.wait_ge(zero_ready, 1)
            sp.dma_start(states[ZROW:ZROW + 1, :], zrow[:, :]).then_inc(zero_stored, 16)

            for ph in range(3):
                def edge(i, s, b, load=True):
                    if load:
                        for h, (g0, g1) in enumerate(PARTS):
                            sp.wait_ge(gathered[ph][s][h], i * (16 * (g1 - g0)) + 16 * (g1 - g0))
                        sp.dma_start(src_idx[:, s, :], src[:, bass.ds((b + 2) * G, G)]).then_inc(idx_loaded[s], 16)
                    for h, (g0, g1) in enumerate(PARTS):
                        sp.wait_ge(step_done, b * G + (ph * T + 2 * G + 1 + g1))
                        if load and ph == 0 and h == 1:
                            sp.wait_ge(w_ready, b * NG + NG + 2)
                            sp.dma_start(ea_sb[:, s, :], ea[:, bass.ds(b + 2, 1), :].rearrange("a b c -> a (b c)")
                                         ).then_inc(ea_loaded[s], 16)
                        sp.dma_start(states_v[:, bass.ds(b, 1), g0 * D:g1 * D].rearrange("p b c -> p (b c)"),
                                     flat(run[:, s, g0:g1])).then_inc(run_stored[s][h], 16)
                    if ph == 0 and s == 0:
                        sp.wait_ge(pre_copied, i + 2)
                        sp.dma_start(self_tab[0][:, bass.ds(i * (CS * D), CS * D)], flat(pre_sb[:, :, :])).then_inc(pre_stored, 16)
                        if load:
                            sp.dma_start(xT_sb[0:D, :], xT[:, bass.ds((i + 1) * (CS * P), CS * P)]).then_inc(xT_loaded, 16)

                in_pairs(sp, NB, edge, lambda i, s, b: edge(i, s, b, False))
                if ph < 2:
                    for s in range(2):
                        for h, (g0, g1) in enumerate(PARTS):
                            sp.wait_ge(gathered[ph][s][h], 16 * (g1 - g0) * TURNS)
                        sp.dma_start(src_idx[:, s, :], src[:, s * G:(s + 1) * G]).then_inc(idx_loaded[s], 16)

                def load_nodes(s, j):
                    sp.dma_start(flat(self_in[:, s]), self_tab[ph][:, bass.ds(j * (C * D), C * D)]).then_inc(node_in[s], 16)
                    if ph != 1:
                        x_in = x_pm if ph == 0 else x1_tab
                        sp.dma_start(flat(res_in[:, s]), x_in[:, bass.ds(j * (C * D), C * D)]).then_inc(node_in[s], 16)

                def node(i, s, j, load=True):
                    sp.wait_ge(node_ready, j + (ph * NC + 1))
                    if load:
                        load_nodes(s, j + 2)
                    if ph != 1:
                        x_out = x1_tab if ph == 0 else out
                        sp.dma_start(x_out[:, bass.ds(j * (C * D), C * D)], flat(node_new[:, s])).then_inc(new_stored[s], 16)
                    if ph < 2:
                        sp.wait_ge(m_copied, j + (ph * NC + 2))
                        sp.dma_start(m_tab_v[ph][:, bass.ds(j * C, C), :], m_sb[:, s]).then_inc(m_stored[s], 16)
                        sp.wait_ge(self_copied, j + (ph * NC + 2))
                        sp.dma_start(self_tab[ph + 1][:, bass.ds(j * (C * D), C * D)], flat(self_out[:, s])).then_inc(self_stored[s], 16)

                half = 16 * (NC // 2)
                if ph == 0:
                    sp.wait_ge(pre_stored, 16 * TURNS + 16)
                for s in range(2):
                    if ph:
                        sp.wait_ge(self_stored[s], half * ph + 16)
                    if ph == 2:
                        sp.wait_ge(new_stored[s], half + 16)
                for s in range(2):
                    load_nodes(s, s)
                in_pairs(sp, NC, node, lambda i, s, j: node(i, s, j, False))
            for s in range(2):
                sp.wait_ge(new_stored[s], half * 2 + 16)

        @block.gpsimd
        def _(pool):
            pool.memset(ones[:, :], 1.0).then_inc(prep, 1)
            pool.iota(iota_i[:, :], [[1, P]], base=0, channel_multiplier=0)
            pool.iota(head_base_i[:, :], [[1, 1]], base=-1, channel_multiplier=T)
            pool.wait_ge(prep, 1)
            pool.affine_select(out=ident[:, :], in_=ones[:, :], compare_op=ALU.is_equal, fill=0.0, base=0,
                               pattern=[[-1, P]], channel_multiplier=1)
            pool.affine_select(out=upper[:, :], in_=ones[:, :], compare_op=ALU.is_ge, fill=0.0, base=0,
                               pattern=[[1, P]], channel_multiplier=-1).then_inc(consts_made, 1)

            for ph in range(3):
                table = x_rows if ph == 0 else m_tab[ph - 1]
                if ph:
                    for s in range(2):
                        pool.wait_ge(m_stored[s], 16 * (NC // 2) * ph + 16)

                def gather(i, s, b):
                    pool.wait_ge(idx_loaded[s], i * 16 + (ph * 16 * (NB // 2) + 16))
                    pool.wait_ge(step_done, b * G + (ph * T + G + 1))
                    pool.sem_inc(turn_begun, 1)
                    for g in range(G):
                        pool.indirect_dma_start(ring[:, s, g, :], None, table,
                                                bass.IndirectOffsetOnAxis(src_idx[:, s, g:g + 1], 0)
                                                ).then_inc(gathered[ph][s][g >= PARTS[1][0]], 16)

                in_pairs(pool, NB, gather)

                for s in range(2):
                    for h in range(2):
                        pool.wait_ge(run_stored[s][h], 16 * TURNS * (ph + 1) + 16)
                pool.wait_ge(tables_ready, 1)
                pool.wait_ge(zero_stored, 16)
                pool.indirect_dma_start(head_rows[:, :], None, states,
                                        bass.IndirectOffsetOnAxis(head_idx[:, 0:1], 0)).then_inc(head_got, 16)
                pool.wait_ge(head_ready, ph + 1)
                pool.indirect_dma_start(states, bass.IndirectOffsetOnAxis(head_idx[:, 0:1], 0),
                                        head_fixed[:, :], None).then_inc(head_put, 16)
                pool.wait_ge(head_put, 16 * (ph + 1))

                def node_gather(i, s, j):
                    pool.wait_ge(end_ready, j + (ph * (NC + 2) + 1))
                    pool.wait_ge(aggT_copied, j + (ph * NC + 1))
                    pool.sem_inc(turn_begun, 1)
                    for c in range(C):
                        pool.indirect_dma_start(agg[:, s, c, :], None, states,
                                                bass.IndirectOffsetOnAxis(end_slot[:, s, c:c + 1], 0)
                                                ).then_inc(agg_gathered[s], 16)

                in_pairs(pool, NC, node_gather)

        @block.tensor
        def _(pe):
            pe.wait_ge(weights_loaded, 16 * 6)
            pe.wait_ge(tables_ready, 2)

            pe.wait_ge(consts_made, 1)
            pe.wait_ge(ends_ready, 1)
            for n in range(2):
                mm = nc.tensor.matmul(ps_ms[1][0:D, n * P:(n + 1) * P], ends_b[:, n, :], ident[:, :], start=True, stop=True)
            mm.then_inc(rows_ready, 1)

            def hidden(i, s, b, g):
                bank = (s * NG + g) % 2
                pe.wait_ge(h_copied, b * NG + (g + 1))
                nc.tensor.matmul(ps_h[bank][0:D, :], w1z_sb[:, g, :], ea_sb[:, s, :], start=True, stop=True
                                 ).then_inc(h_ready, 1)

            def weight(i, s, b, g):
                bank = (s * NG + g) % 2
                pe.wait_ge(h_copied, b * NG + (g + 3))
                pe.wait_ge(msg_done, b * NG + (g + 1))
                for q in range(GQ):
                    mm = nc.tensor.matmul(ps_w[bank][:, q * D:(q + 1) * D], hT[:, bank, q * P:(q + 1) * P],
                                          w2a_sb[:, :], start=True, stop=True)
                mm.then_inc(w_ready, 1)

            def edge(i, s, b):
                pe.wait_ge(ea_loaded[s], i * 16 + 16)
                hidden(i, s, b, 0)
                for g in range(1, NG):
                    hidden(i, s, b, g)
                    weight(i, s, b, g - 1)
                weight(i, s, b, NG - 1)
                pe.wait_ge(hot_ready, b + 1)
                for g in range(G):
                    mm = nc.tensor.matmul(ps_hist[:, 0:NBLK], hot_lo[:, g, :], hot_hi[:, g, :],
                                          start=False, stop=False, skip_group_check=True)
                mm.then_inc(hist_added, 1)
                if s == 0:
                    pe.wait_ge(xT_loaded, i * 16 + 16)
                    pe.wait_ge(pre_copied, i + 1)
                    for c in range(CS):
                        mm = nc.tensor.matmul(ps_pre[:, c * D:(c + 1) * D], xT_sb[:, c * P:(c + 1) * P], wsa_sb[:, :],
                                              start=True, stop=True)
                    mm.then_inc(pre_ready, 1)

            nc.tensor.matmul(ps_hist[:, 0:NBLK], zeros_w[:, :], zeros_w[:, 0:NBLK], start=True, stop=False, skip_group_check=True)
            in_pairs(pe, NB, edge)

            pe.wait_ge(hist_copied, 1)
            nc.tensor.matmul(ps_ms[1][:, 0:NBLK], upper[:, :], hist[:, :], start=True, stop=True)
            nc.tensor.matmul(ps_ms[1][:, P:P + NBLK], ones[:, :], hist[:, :], start=True, stop=True).then_inc(hist_summed, 1)

            for ph in range(3):
                pe.wait_ge(step_done, (ph + 1) * T + 2 * G + 1)
                pe.transpose(ps_t[0][0:D, 0:P], run[:, 1, G - 1, :], ident[:, :]).then_inc(last_T, 1)
                pe.wait_ge(carry_ready, ph + 1)
                pe.transpose(ps_t[1][:, 0:D], carry_in[:, :], ident[0:D, 0:D]).then_inc(carry_back, 1)
                pe.wait_ge(head_ready, ph + 1)

                def agg_transposes(i, s, j):
                    pe.wait_ge(agg_gathered[s], i * (16 * C) + (ph * 16 * C * (NC // 2) + 16 * C))
                    if ph < 2:
                        pe.wait_ge(nodeT_copied, j + (ph * NC + 1))
                    for c in range(C):
                        mm = pe.transpose(ps_t[c // 4][0:D, (c % 4) * P:(c % 4 + 1) * P], agg[:, s, c, :], ident[:, :])
                    mm.then_inc(aggT_ready, 1)

                def agg_products(i, s, j):
                    pe.wait_ge(aggT_copied, j + (ph * NC + 3))
                    pe.wait_ge(o_used, j + (ph * NC + 1))
                    for c in range(C):
                        mm = nc.tensor.matmul(ps_o[c // 4][:, (c % 4) * D:(c % 4 + 1) * D], aggT[:, s, c * P:(c + 1) * P],
                                              wn_sb[:, ph, :], start=True, stop=True)
                    mm.then_inc(o_ready, 1)

                def node_transposes(i, s, j):
                    pe.wait_ge(node_ready, j + (ph * NC + 1))
                    for c in range(C):
                        mm = pe.transpose(ps_t[c // 4][0:D, (c % 4) * P:(c % 4 + 1) * P], node_new[:, s, c, :], ident[:, :])
                    mm.then_inc(nodeT_ready, 1)

                def node_products(i, s, j):
                    pe.wait_ge(nodeT_copied, j + (ph * NC + 3))
                    pe.wait_ge(m_copied, j + (ph * NC + 1))
                    pe.wait_ge(self_copied, j + (ph * NC + 1))
                    for c in range(C):
                        mm = nc.tensor.matmul(ps_ms[c // 2][:, (c % 2) * 2 * D:(c % 2 + 1) * 2 * D],
                                              nodeT[:, s, c * P:(c + 1) * P], wpsa_sb[:, ph, :], start=True, stop=True)
                    mm.then_inc(ms_ready, 1)

                def both(i, s, j):
                    node_transposes(i, s, j)
                    agg_transposes(i + 1, s, j + 2)
                    node_products(i, s, j)
                    agg_products(i + 1, s, j + 2)

                def nodes_only(i, s, j):
                    node_transposes(i, s, j)
                    node_products(i, s, j)

                def agg_only(i, s, j):
                    agg_transposes(i, s, j)
                    agg_products(i, s, j)

                if ph < 2:
                    for s in range(2):
                        agg_only(0, s, s)
                    in_pairs(pe, NC, both, nodes_only)
                else:
                    in_pairs(pe, NC, agg_only)

        @block.scalar
        def _(act):
            act.wait_ge(weights_loaded, 16 * 6)
            act.wait_ge(tables_ready, 2)

            def edge(i, s, b):
                for g in range(NG):
                    bank = (s * NG + g) % 2
                    act.wait_ge(h_ready, b * NG + (g + 1))
                    act.wait_ge(w_ready, b * NG + (g + 1))
                    nc.scalar.activation(hT[0:D, bank, :], ps_h[bank][0:D, :], ACT.Relu, bias=b1_sb[:, 0:1]
                                         ).then_inc(h_copied, 1)
                if s == 0:
                    act.wait_ge(pre_ready, i + 1)
                    act.wait_ge(pre_stored, i * 16 + 16)
                    nc.scalar.activation(flat(pre_sb[:, :, :]), ps_pre[:, 0:CS * D], ACT.Copy).then_inc(pre_copied, 1)

            in_pairs(act, NB, edge)

            for ph in range(3):
                def root(j, eps):
                    act.wait_ge(var_in, j)
                    nc.scalar.activation(stat[:, 1, :], root_in(eps), ACT.Sqrt, bias=eps[:, 0:1]).then_inc(std_ready, 1)

                def root_in(eps):
                    return mean_var[:, :, 1] if eps is eps_col else stat[:, 0, :]

                def copy_agg(i, s, j):
                    act.wait_ge(aggT_ready, j + (ph * NC + 1))
                    nc.scalar.activation(aggT[:, s, 0:4 * P], ps_t[0][0:D, :], ACT.Copy)
                    nc.scalar.activation(aggT[:, s, 4 * P:C * P], ps_t[1][0:D, 0:(C - 4) * P], ACT.Copy).then_inc(aggT_copied, 1)
                    nc.scalar.activation(end_slot[:, s, :], end_idx[:, bass.ds((j + 2) * C, C)], ACT.Copy).then_inc(end_ready, 1)

                def copy_nodes(i, s, j):
                    act.wait_ge(nodeT_ready, j + (ph * NC + 1))
                    nc.scalar.activation(nodeT[0:D, s, 0:4 * P], ps_t[0][0:D, :], ACT.Copy)
                    nc.scalar.activation(nodeT[0:D, s, 4 * P:C * P], ps_t[1][0:D, 0:(C - 4) * P], ACT.Copy).then_inc(nodeT_copied, 1)

                def copy_products(i, s, j):
                    act.wait_ge(ms_ready, j + (ph * NC + 1))
                    act.wait_ge(m_stored[s], i * 16 + (ph * 16 * (NC // 2) + 16))
                    ms = [ps_ms[q][:, 0:min(2, C - 2 * q) * 2 * D].rearrange("p (w d) -> p w d", d=2 * D) for q in range(4)]
                    for q in range(4):
                        last = nc.scalar.activation(m_sb[:, s, 2 * q:min(2 * q + 2, C), :], ms[q][:, :, 0:D],
                                                    ACT.Relu, bias=zero_col[:, 0:1])
                    last.then_inc(m_copied, 1)
                    act.wait_ge(self_stored[s], i * 16 + (ph * 16 * (NC // 2) + 16))
                    for q in range(4):
                        last = nc.scalar.activation(self_out[:, s, 2 * q:min(2 * q + 2, C), :], ms[q][:, :, D:2 * D], ACT.Copy)
                    last.then_inc(self_copied, 1)

                if ph < 2:
                    eps = eps_col if ph == 0 else zero_col

                    def both(i, s, j):
                        copy_nodes(i, s, j)
                        copy_agg(i + 1, s, j + 2)
                        root(j + (ph * NC + 2), eps)
                        copy_products(i, s, j)

                    def tail(i, s, j):
                        copy_nodes(i, s, j)
                        if j < NC - 1:
                            root(j + (ph * NC + 2), eps)
                        copy_products(i, s, j)

                    copy_agg(0, 0, 0)
                    copy_agg(0, 1, 1)
                    root(ph * NC + 1, eps)
                    in_pairs(act, NC, both, tail)
                else:
                    def roots(i, s, j, ahead=True):
                        if ahead:
                            copy_agg(i + s, 1 - s, j + 1)
                        root(j * 2 + (2 * NC + 1), zero_col)
                        root(j * 2 + (2 * NC + 2), eps_col)

                    copy_agg(0, 0, 0)
                    in_pairs(act, NC, roots, lambda i, s, j: roots(i, s, j, j < NC - 1))

        @block.vector
        def _(dve):
            done = [0]

            def chain(ins):
                done[0] += 1
                ins.then_inc(end_step, 1)
                dve.wait_ge(end_step, done[0])

            v = nc.vector
            chain(v.memset(run[:, 1, G - 1, :], 0.0))
            v.memset(zrow[:, :], 0.0).then_inc(zero_ready, 1)
            v.memset(zeros_w[:, :], 0.0)
            v.memset(eps_col[:, :], LN_EPS)
            v.memset(zero_col[:, :], 0.0)
            v.memset(nodeT[D:D1, :, :], 1.0)
            v.memset(xT_sb[D:D + 2, :], 1.0)
            v.memset(carry[:, 0:1], 0.0)
            v.memset(cont_row[:, 0:1], 0.0)
            v.memset(keep[:, 0:1], 0.0)
            v.memset(end_idx[:, NBLK:], 0)
            v.memset(hT[D:D1, :, :], 1.0)
            v.memset(head_rows[:, 0:1], 0.0).then_inc(tables_ready, 2)

            dve.wait_ge(dst_loaded, 16)
            dve.wait_ge(consts_made, 1)
            v.tensor_copy(ends_f[:, 0:1], dst_i[:, 0:1])
            chain(v.tensor_copy(ends_f[:, 1:2], dst_i[:, T - 1:T]))
            v.tensor_scalar(ends_b[:, 0, :], ones[:, 0:D], ends_f[:, 0:1], None, ALU.mult)
            v.tensor_scalar(ends_b[:, 1, :], ones[:, 0:D], ends_f[:, 1:2], None, ALU.mult).then_inc(ends_ready, 1)
            v.tensor_tensor(keep[:, 1:T], dst_i[:, 1:T], dst_i[:, 0:T - 1], ALU.is_equal)
            v.tensor_scalar(dst_hi_i[:, :], dst_i[:, :], 7, None, ALU.arith_shift_right)
            chain(v.tensor_scalar(dst_lo_i[:, :], dst_i[:, :], P - 1, None, ALU.bitwise_and))
            v.tensor_copy(dst_hi[:, :], dst_hi_i[:, :])
            v.tensor_copy(dst_lo[:, :], dst_lo_i[:, :])
            v.tensor_copy(head_base[:, :], head_base_i[:, :])
            v.tensor_copy(iota[:, :], iota_i[:, :])
            chain(v.tensor_scalar(same_first[:, :], dst_i[:, :], ends_f[:, 0:1], None, ALU.is_equal))
            chain(v.tensor_reduce(head_n[:, :], same_first[:, :], AX.X, ALU.add))
            v.tensor_tensor(head_idx[:, :], head_n[:, :], head_base[:, :], ALU.add)
            dve.wait_ge(rows_ready, 1)
            chain(v.tensor_copy(last_row[:, :], ps_ms[1][0:D, P:2 * P]))
            v.tensor_tensor(cont_row[:, 1:P], ps_ms[1][0:D, 1:P], last_row[:, 0:P - 1], ALU.is_equal)
            chain(v.tensor_tensor(whole_row[:, :], ps_ms[1][0:D, 0:P], last_row[:, :], ALU.is_equal))
            chain(v.tensor_tensor(pass_row[:, :], whole_row[:, :], cont_row[:, :], ALU.mult))

            for ph in range(3):
                merge = ALU.add if ph == 0 else ALU.max

                def edge(i, s, b):
                    dve.wait_ge(step_done, b * G + (ph * T + G + 1))
                    v.tensor_scalar(keep_b[:, s, :], keep[:, bass.ds(b * G, G)], 0.0, None, ALU.add).then_inc(keep_copied, 1)
                    if ph == 0:
                        dve.wait_ge(hist_added, b + 1)
                        v.tensor_tensor(hot_hi[:, :, :], iota[:, 0:NBLK].unsqueeze(1).to_broadcast([P, G, NBLK]),
                                        dst_hi[:, bass.ds(b * G, G)].unsqueeze(2).to_broadcast([P, G, NBLK]), ALU.is_equal)
                        v.tensor_tensor(hot_lo[:, :, :], iota[:, :].unsqueeze(1).to_broadcast([P, G, P]),
                                        dst_lo[:, bass.ds(b * G, G)].unsqueeze(2).to_broadcast([P, G, P]), ALU.is_equal
                                        ).then_inc(hot_ready, 1)
                    dve.wait_ge(keep_copied, b + (ph * NB + 1))
                    for g in range(G):
                        for h, (g0, g1) in enumerate(PARTS):
                            if g == g0:
                                dve.wait_ge(gathered[ph][s][h], i * (16 * (g1 - g0)) + 16 * (g1 - g0))
                                dve.wait_ge(run_stored[s][h], i * 16 + (ph * 16 * TURNS + 16))
                        if ph == 0 and g % GQ == 0:
                            n = g // GQ
                            dve.wait_ge(w_ready, b * NG + (n + 3))
                            v.tensor_tensor(flat(ring[:, s, g:g + GQ]), ps_w[(s * NG + n) % 2][:, 0:GQ * D],
                                            flat(ring[:, s, g:g + GQ]), ALU.mult).then_inc(msg_done, 1)
                            dve.wait_ge(msg_done, b * NG + (n + 3))
                        before = run[:, s, g - 1, :] if g else run[:, 1 - s, G - 1, :]
                        dve.wait_ge(step_done, b * G + (ph * T + 2 * G + 1 + g))
                        v.scalar_tensor_tensor(run[:, s, g, :], before, keep_b[:, s, g:g + 1], ring[:, s, g, :],
                                               ALU.mult, merge).then_inc(step_done, 1)

                in_pairs(dve, NB, edge)

                if ph == 0:
                    dve.wait_ge(hist_added, NB + 1)
                    v.tensor_copy(hist[:, :], ps_hist[:, 0:NBLK]).then_inc(hist_copied, 1)
                dve.wait_ge(last_T, ph + 1)
                v.tensor_tensor_scan(carry[:, 1:P + 1], pass_row[:, :], ps_t[0][0:D, 0:P], 0.0, ALU.mult, merge
                                     ).then_inc(carried, 1)
                dve.wait_ge(carried, ph + 1)
                v.tensor_tensor(carry_in[:, :], cont_row[:, :], carry[:, 0:P], ALU.mult).then_inc(carry_ready, 1)
                if ph == 0:
                    dve.wait_ge(hist_summed, 1)
                    chain(v.tensor_tensor_scan(nodes_cum[:, :], ones[:, 0:NBLK], ps_ms[1][:, P:P + NBLK], 0.0, ALU.mult, ALU.add))
                    chain(v.tensor_tensor(end_a[:, :], nodes_cum[:, :], ps_ms[1][:, P:P + NBLK], ALU.subtract))
                    chain(v.tensor_tensor(end_b[:, :], ps_ms[1][:, 0:NBLK], end_a[:, :], ALU.add))
                    v.tensor_scalar(end_a[:, :], end_b[:, :], -float(ZROW + 1), None, ALU.add)
                    chain(v.tensor_scalar(some[:, :], hist[:, :], 0.0, None, ALU.is_gt))
                    chain(v.tensor_tensor(end_b[:, :], end_a[:, :], some[:, :], ALU.mult))
                    chain(v.tensor_scalar(end_idx[:, 0:NBLK], end_b[:, :], float(ZROW), None, ALU.add))
                for s in range(2):
                    v.tensor_copy(end_slot[:, s, :], end_idx[:, s * C:(s + 1) * C]).then_inc(end_ready, 1)
                dve.wait_ge(head_got, 16 * (ph + 1))
                dve.wait_ge(carry_back, ph + 1)
                v.tensor_tensor(head_fixed[:, :], ps_t[1][:, 0:D], head_rows[:, :], merge).then_inc(head_ready, 1)

                n_in = 32 if ph != 1 else 16
                base_in = [0, 32 * (NC // 2), 48 * (NC // 2)][ph]
                n_steps = [4, 5, 7][ph]
                base_steps = [0, 4 * NC, 9 * NC][ph]

                def first(i, s, j):
                    at = [0]

                    def link(ins):
                        at[0] += 1
                        ins.then_inc(node_step, 1)
                        dve.wait_ge(node_step, j * n_steps + (base_steps + at[0]))

                    def wide(k):
                        return stat[:, k, :].unsqueeze(2).to_broadcast([P, C, D])

                    def layer_norm(out_ap, n):
                        for c in range(C):
                            last = v.bn_stats(bn[:, c, :], t1[:, c, :])
                        link(last)
                        v.memset(scratch[:, 1:2], 0.0)
                        for c in range(C):
                            last = v.bn_aggr(mean_var[:, c, :], bn[:, c, :])
                        last.then_inc(var_in, 1)
                        dve.wait_ge(std_ready, n)
                        link(v.reciprocal(stat[:, 2, :], stat[:, 1, :]))
                        for c in range(C):
                            last = v.tensor_scalar(out_ap[:, c, :], t1[:, c, :], mean_var[:, c, 0:1], stat[:, 2, c:c + 1],
                                                   ALU.subtract, ALU.mult)
                        last.then_inc(node_ready, 1)

                    def l2_scale(n):
                        link(v.tensor_tensor(sq[:, :, :], t2[:, :, :], t2[:, :, :], ALU.mult))
                        v.tensor_reduce(stat[:, 0, :], sq[:, :, :], AX.X, ALU.add).then_inc(var_in, 1)
                        dve.wait_ge(std_ready, n)
                        link(v.tensor_scalar(stat[:, 0, :], stat[:, 1, :], L2_EPS, None, ALU.max))
                        link(v.reciprocal(stat[:, 2, :], stat[:, 0, :]))

                    dve.wait_ge(o_ready, j + (ph * NC + 1))
                    dve.wait_ge(node_in[s], i * n_in + (base_in + n_in))
                    before = t2 if ph == 2 else t1
                    v.tensor_tensor(flat(before[:, 0:4]), ps_o[0][:, 0:4 * D], flat(self_in[:, s, 0:4]), ALU.add)
                    link(v.tensor_tensor(flat(before[:, 4:C]), ps_o[1][:, 0:(C - 4) * D], flat(self_in[:, s, 4:C]), ALU.add))
                    v.memset(scratch[:, 0:1], 0.0).then_inc(o_used, 1)
                    if ph == 0:
                        link(v.scalar_tensor_tensor(t1[:, :, :], t1[:, :, :], 0.0, res_in[:, s], ALU.max, ALU.add))
                        dve.wait_ge(new_stored[s], i * 16 + 16)
                        layer_norm(node_new[:, s], j + 1)
                    elif ph == 1:
                        link(v.tensor_scalar(t2[:, :, :], t1[:, :, :], 0.0, None, ALU.max))
                        l2_scale(j + (NC + 1))
                        v.tensor_tensor(node_new[:, s], t2[:, :, :], wide(2), ALU.mult).then_inc(node_ready, 1)
                    else:
                        l2_scale(j * 2 + (2 * NC + 1))
                        for c in range(C):
                            last = v.scalar_tensor_tensor(t1[:, c, :], t2[:, c, :], stat[:, 2, c:c + 1], res_in[:, s, c, :],
                                                          ALU.mult, ALU.add)
                        link(last)
                        dve.wait_ge(new_stored[s], i * 16 + (16 * (NC // 2) + 16))
                        layer_norm(node_new[:, s], j * 2 + (2 * NC + 2))
                    assert at[0] == n_steps
                    dve.wait_ge(node_ready, j + (ph * NC + 1))

                in_pairs(dve, NC, first)


def kernel(**inputs):
    from concourse import bacc
    from concourse.bass_utils import run_bass_kernel_spmd

    a = {k: np.asarray(v) for k, v in inputs.items()}
    f32, i32 = np.float32, np.int32

    def rows(x, n, fill=0):
        pad = np.full((n - x.shape[0],) + x.shape[1:], fill, x.dtype)
        return np.concatenate([x, pad])

    src = rows(a["src"], EP).reshape(P, T)
    dst = rows(a["dst"], EP, NP).reshape(P, T)
    ea = rows(a["edge_attr_17"], EP).reshape(P, NB, NG, GQ, ED).transpose(2, 4, 1, 3, 0).reshape(NG * ED, NB, GQ * P)
    x = rows(a["x"], NP)
    x_pm = x.reshape(NBLK, P, D).transpose(1, 0, 2).reshape(P, NBLK * D)
    w1z = np.zeros((NG * ED, NG, D), f32)
    for g in range(NG):
        w1z[g * ED:(g + 1) * ED, g] = a["L0_gnn_W1"].T
    w2a = np.concatenate([a["L0_gnn_W2"].T, a["L0_gnn_b2"][None]])
    wsa = np.concatenate([a["L0_gnn_Ws"].T, a["L0_gnn_bs"][None], a["L0_gnn_bn"][None]])
    wn = np.stack([a["L0_gnn_Wn"].T, a["L1_gnn_Wn1"], a["L1_gnn_Wn2"]], 1)
    wpsa = np.stack([np.concatenate([np.concatenate([a[f"L1_gnn_Wp{n}"], a[f"L1_gnn_bp{n}"][None]]),
                                     np.concatenate([a[f"L1_gnn_Ws{n}"], a[f"L1_gnn_b{n}"][None]])], 1) for n in (1, 2)], 1)
    arrays = {"src": src, "dst": dst, "ea": ea, "x_pm": x_pm, "xT": rows(x, TURNS * CS * P).T, "w1z": w1z,
              "b1": a["L0_gnn_b1"][:, None], "w2a": w2a, "wsa": wsa, "wn": wn, "wpsa": wpsa, "x_rows": x}
    arrays = {k: np.ascontiguousarray(v) for k, v in arrays.items()}
    nc = bacc.Bacc("TRN2", target_bir_lowering=False, num_devices=1)
    aps = {k: nc.dram_tensor(k, v.shape, mybir.dt.from_np(v.dtype), kind="ExternalInput").ap() for k, v in arrays.items()}
    out = nc.dram_tensor("out", (P, NBLK * D), F32, kind="ExternalOutput").ap()
    build(nc, **aps, out=out)
    r = run_bass_kernel_spmd(nc, [arrays], core_ids=[0])
    got = np.asarray(r.results[0]["out"])
    return got.reshape(P, NBLK, D).transpose(1, 0, 2).reshape(NP, D)[:N]
```

```python
from contextlib import ExitStack

import numpy as np

import concourse.bass as bass
from concourse import mybir

ALU = mybir.AluOpType
ACT = mybir.ActivationFunctionType
AX = mybir.AxisListType
F32 = mybir.dt.float32
BF16 = mybir.dt.bfloat16
I32 = mybir.dt.int32

P = 128
N, E, D, ED = 12500, 200000, 96, 17

T = -(-E // P)
EP = P * T
G = 28
NB = -(-T // G)
GL = T - (NB - 1) * G
assert NB % 2 == 0
GQ = 4
NG = G // GQ
assert NG * ED <= P
HALF = 20
assert HALF % GQ == 0 and HALF < GL

NBLK = -(-N // P)
NP = NBLK * P
C = 7
SHORT = [7, 6, 5, 4, 4, 2]
SIZES = [C] * ((NBLK - sum(SHORT)) // C) + SHORT
NC = len(SIZES)
assert sum(SIZES) == NBLK and NC % 2 == 0
PEEL = len(SHORT) // 2 + 2
ZROW = EP
TURNS = NB // 2
CS = 4
assert CS * TURNS >= NBLK
D1 = D + 1

LN_EPS = 1e-5
L2_EPS = 1e-12


def parts(steps):
    return [(0, HALF), (HALF, steps)]


def steps_of(b):
    return GL if among_last(b, NB, 1) else G


def among_last(j, n, k):
    return isinstance(j, int) and j >= n - k


def size(j):
    return SIZES[j] if isinstance(j, int) else C


def start(j):
    return sum(SIZES[:j]) if isinstance(j, int) else j * C


def gathered_blocks(i, s, j):
    return sum(SIZES[s:j:2]) if isinstance(j, int) else i * C


def build_by_partition(nc, ctx, src, dst, ea, x_rows, x_pm, xT, w1z, b1, w2a, wsa, wn, wpsa, out):
    def sb(name, shape, dt=F32):
        return ctx.enter_context(nc.sbuf_tensor(name, shape, dt))

    def sem(name):
        return ctx.enter_context(nc.semaphore(name))

    def sem2(name):
        return [sem(f"{name}{s}") for s in range(2)]

    states = nc.dram_tensor("states", (EP + 1, D), F32).ap()
    states_v = states[0:EP, :].rearrange("(p t) d -> p (t d)", p=P)
    m_tab = [nc.dram_tensor(f"m_tab{i}", (NP, D), F32).ap() for i in range(2)]
    m_tab_v = [m.rearrange("(k p) d -> p k d", p=P) for m in m_tab]
    self_tab = [nc.dram_tensor(f"self_tab{i}", (P, (TURNS * CS if i == 0 else NBLK) * D), F32).ap()
                for i in range(3)]
    x1_tab = nc.dram_tensor("x1_tab", (P, NBLK * D), F32).ap()

    src_idx = sb("src_idx", [P, 2, G], I32)
    ring = sb("ring", [P, 2, G, D])
    run = sb("run", [P, 2, G, D])
    dst_i = sb("dst_i", [P, T], I32)
    dst_hi_i = sb("dst_hi_i", [P, T], I32)
    dst_lo_i = sb("dst_lo_i", [P, T], I32)
    dst_hi = sb("dst_hi", [P, T], BF16)
    dst_lo = sb("dst_lo", [P, T], BF16)
    keep = sb("keep", [P, T])
    keep_b = sb("keep_b", [P, 2, G])
    zeros_w = sb("zeros_w", [P, P], BF16)
    iota_i = sb("iota_i", [P, P], I32)
    iota = sb("iota", [P, P], BF16)
    hot_hi = sb("hot_hi", [P, G, NBLK], BF16)
    hot_lo = sb("hot_lo", [P, G, P], BF16)
    ea_sb = sb("ea_sb", [NG * ED, 2, GQ * P])
    hT = sb("hT", [D1, 2, GQ * P])
    w1z_sb = sb("w1z_sb", [NG * ED, NG, D])
    b1_sb = sb("b1_sb", [D, 1])
    w2a_sb = sb("w2a_sb", [D1, D])
    ident = sb("ident", [P, P])
    upper = sb("upper", [P, P])
    ones = sb("ones", [P, P])
    ends_f = sb("ends_f", [P, 2])
    ends_b = sb("ends_b", [P, 2, D])
    last_row = sb("last_row", [D, P])
    whole_row = sb("whole_row", [D, P])
    cont_row = sb("cont_row", [D, P])
    pass_row = sb("pass_row", [D, P])
    same_first = sb("same_first", [P, T])
    head_n = sb("head_n", [P, 1])
    head_base_i = sb("head_base_i", [P, 1], I32)
    head_base = sb("head_base", [P, 1])
    head_idx = sb("head_idx", [P, 1], I32)
    carry = sb("carry", [D, P + 1])
    carry_in = sb("carry_in", [D, P])
    head_rows = sb("head_rows", [P, D])
    head_fixed = sb("head_fixed", [P, D])
    hist = sb("hist", [P, NBLK])
    nodes_cum = sb("nodes_cum", [P, NBLK])
    end_a = sb("end_a", [P, NBLK])
    end_b = sb("end_b", [P, NBLK])
    some = sb("some", [P, NBLK])
    end_idx = sb("end_idx", [P, NBLK + 2 * C], I32)
    end_slot = sb("end_slot", [P, 2, C], I32)
    agg = sb("agg", [P, 2, C, D])
    aggT = sb("aggT", [D, 2, C * P])
    self_in = sb("self_in", [P, 2, C, D])
    res_in = sb("res_in", [P, 2, C, D])
    t1 = sb("t1", [P, C, D])
    t2 = sb("t2", [P, C, D])
    sq = sb("sq", [P, C, D])
    stat = sb("stat", [P, 3, C])
    bn = sb("bn", [P, C, 6])
    mean_var = sb("mean_var", [P, C, 2])
    scratch = sb("scratch", [P, 2])
    node_new = sb("node_new", [P, 2, C, D])
    nodeT = sb("nodeT", [D1, 2, C * P])
    xT_sb = sb("xT_sb", [D + 2, CS * P])
    pre_sb = sb("pre_sb", [P, CS, D])
    m_sb = sb("m_sb", [P, 2, C, D])
    self_out = sb("self_out", [P, 2, C, D])
    wsa_sb = sb("wsa_sb", [D + 2, D])
    wn_sb = sb("wn_sb", [D, 3, D])
    wpsa_sb = sb("wpsa_sb", [D1, 2, 2 * D])
    eps_col = sb("eps_col", [P, 1])
    zero_col = sb("zero_col", [P, 1])
    zrow = sb("zrow", [1, D])

    ps = [ctx.enter_context(nc.psum_tensor(f"ps{i}", [P, 512], F32)) for i in range(8)]
    ps_h, ps_w, ps_hist, ps_pre = ps[0:2], ps[2:4], ps[4], ps[6]
    ps_t, ps_o, ps_ms = ps[0:2], ps[2:4], ps[4:8]

    s_credit = sem("s_credit")
    idx_loaded = sem2("idx_loaded")
    dst_loaded, weights_loaded = sem("dst_loaded"), sem("weights_loaded")
    ea_loaded, xT_loaded = sem2("ea_loaded"), sem("xT_loaded")
    gathered = [[sem2(f"gathered{ph}_{s}_") for s in range(2)] for ph in range(3)]
    turn_begun = sem("turn_begun")
    step_done = sem("step_done")
    run_stored = [sem2(f"run_stored{s}_") for s in range(2)]
    h_ready, h_copied, w_ready, msg_done = sem("h_ready"), sem("h_copied"), sem("w_ready"), sem("msg_done")
    hot_ready, hist_added = sem("hot_ready"), sem("hist_added")
    consts_made, prep = sem("consts_made"), sem("prep")
    keep_copied = sem("keep_copied")
    ends_ready, rows_ready = sem("ends_ready"), sem("rows_ready")
    tables_ready = sem("tables_ready")
    last_T, carried, carry_ready, carry_back = sem("last_T"), sem("carried"), sem("carry_ready"), sem("carry_back")
    head_got, head_ready, head_put = sem("head_got"), sem("head_ready"), sem("head_put")
    hist_copied, hist_summed, end_step, end_ready = sem("hist_copied"), sem("hist_summed"), sem("end_step"), sem("end_ready")
    agg_gathered = sem2("agg_gathered")
    aggT_ready, aggT_copied = sem("aggT_ready"), sem("aggT_copied")
    o_ready, o_used = sem("o_ready"), sem("o_used")
    node_step, node_ready = sem("node_step"), sem("node_ready")
    var_in, std_ready = sem("var_in"), sem("std_ready")
    nodeT_ready, nodeT_copied = sem("nodeT_ready"), sem("nodeT_copied")
    ms_ready, m_copied, self_copied = sem("ms_ready"), sem("m_copied"), sem("self_copied")
    node_in, m_stored, self_stored, new_stored = sem2("node_in"), sem2("m_stored"), sem2("self_stored"), sem2("new_stored")
    pre_ready, pre_copied, pre_stored = sem("pre_ready"), sem("pre_copied"), sem("pre_stored")
    zero_ready, zero_stored = sem("zero_ready"), sem("zero_stored")

    def in_pairs(eng, n, body, peel):
        with eng.Fori(0, n // 2 - peel) as i:
            for s in range(2):
                body(i, s, i * 2 + s)
        for i in range(n // 2 - peel, n // 2):
            for s in range(2):
                body(i, s, i * 2 + s)

    def flat(ap):
        return ap.rearrange("p c d -> p (c d)")

    def sync_program(sp):
        sp.sem_inc(step_done, 2 * G + 1)
        sp.sem_inc(h_copied, 2)
        sp.sem_inc(w_ready, 2)
        sp.sem_inc(msg_done, 2)
        sp.sem_inc(hist_added, 1)
        sp.sem_inc(pre_copied, 1)
        sp.sem_inc(pre_stored, 16)
        sp.sem_inc(nodeT_copied, 2)
        sp.sem_inc(aggT_copied, 2)
        sp.sem_inc(o_used, 1)
        sp.sem_inc(m_copied, 1)
        sp.sem_inc(self_copied, 1)
        for s in range(2):
            for h in range(2):
                sp.sem_inc(run_stored[s][h], 16)
            sp.sem_inc(m_stored[s], 16)
            sp.sem_inc(self_stored[s], 16)
            sp.sem_inc(new_stored[s], 16)
        for s in range(2):
            sp.dma_start(src_idx[:, s, :], src[:, s * G:(s + 1) * G]).then_inc(idx_loaded[s], 16)
        sp.dma_start(dst_i[:, :], dst).then_inc(dst_loaded, 16)
        weights = [(wsa_sb[:, :], wsa), (w1z_sb[:, :, :], w1z), (b1_sb[:, :], b1), (w2a_sb[:, :], w2a),
                   (wn_sb[:, :, :], wn), (wpsa_sb[:, :, :], wpsa)]
        for to, of in weights:
            sp.dma_start(to, of).then_inc(weights_loaded, 16)
        for s in range(2):
            sp.dma_start(ea_sb[:, s, :], ea[:, s, :]).then_inc(ea_loaded[s], 16)
        sp.dma_start(xT_sb[0:D, :], xT[:, 0:CS * P]).then_inc(xT_loaded, 16)
        sp.wait_ge(zero_ready, 1)
        sp.dma_start(states[ZROW:ZROW + 1, :], zrow[:, :]).then_inc(zero_stored, 16)

        for ph in range(3):
            def edge(i, s, b):
                load = not among_last(b, NB, 2)
                if load:
                    for h, (g0, g1) in enumerate(parts(G)):
                        sp.wait_ge(gathered[ph][s][h], i * (16 * (g1 - g0)) + 16 * (g1 - g0))
                    sp.dma_start(src_idx[:, s, :], src[:, bass.ds((b + 2) * G, G)]).then_inc(idx_loaded[s], 16)
                for h, (g0, g1) in enumerate(parts(steps_of(b))):
                    sp.wait_ge(step_done, b * G + (ph * T + 2 * G + 1 + g1))
                    if load and ph == 0 and h == 1:
                        sp.wait_ge(w_ready, b * NG + NG + 2)
                        sp.dma_start(ea_sb[:, s, :], ea[:, bass.ds(b + 2, 1), :].rearrange("a b c -> a (b c)")
                                     ).then_inc(ea_loaded[s], 16)
                    sp.dma_start(states_v[:, bass.ds(b * (G * D) + g0 * D, (g1 - g0) * D)],
                                 flat(run[:, s, g0:g1])).then_inc(run_stored[s][h], 16)
                if ph == 0 and s == 0:
                    sp.wait_ge(pre_copied, i + 2)
                    sp.dma_start(self_tab[0][:, bass.ds(i * (CS * D), CS * D)], flat(pre_sb[:, :, :])).then_inc(pre_stored, 16)
                    if load:
                        sp.dma_start(xT_sb[0:D, :], xT[:, bass.ds((i + 1) * (CS * P), CS * P)]).then_inc(xT_loaded, 16)

            in_pairs(sp, NB, edge, 1)
            if ph < 2:
                for s in range(2):
                    for h, (g0, g1) in enumerate(parts(G)):
                        short = G - GL if s == 1 and h == 1 else 0
                        sp.wait_ge(gathered[ph][s][h], 16 * ((g1 - g0) * TURNS - short))
                    sp.dma_start(src_idx[:, s, :], src[:, s * G:(s + 1) * G]).then_inc(idx_loaded[s], 16)

            def load_nodes(s, j):
                n, cols = size(j), bass.ds(start(j) * D, size(j) * D)
                sp.dma_start(flat(self_in[:, s, 0:n]), self_tab[ph][:, cols]).then_inc(node_in[s], 16)
                if ph != 1:
                    x_in = x_pm if ph == 0 else x1_tab
                    sp.dma_start(flat(res_in[:, s, 0:n]), x_in[:, cols]).then_inc(node_in[s], 16)

            def node(i, s, j):
                n, cols = size(j), bass.ds(start(j) * D, size(j) * D)
                sp.wait_ge(node_ready, j + (ph * NC + 1))
                if not among_last(j, NC, 2):
                    load_nodes(s, j + 2)
                if ph != 1:
                    x_out = x1_tab if ph == 0 else out
                    sp.dma_start(x_out[:, cols], flat(node_new[:, s, 0:n])).then_inc(new_stored[s], 16)
                if ph < 2:
                    sp.wait_ge(m_copied, j + (ph * NC + 2))
                    sp.dma_start(m_tab_v[ph][:, bass.ds(start(j), n), :], m_sb[:, s, 0:n]).then_inc(m_stored[s], 16)
                    sp.wait_ge(self_copied, j + (ph * NC + 2))
                    sp.dma_start(self_tab[ph + 1][:, cols], flat(self_out[:, s, 0:n])).then_inc(self_stored[s], 16)

            half = 16 * (NC // 2)
            if ph == 0:
                sp.wait_ge(pre_stored, 16 * TURNS + 16)
            for s in range(2):
                if ph:
                    sp.wait_ge(self_stored[s], half * ph + 16)
                if ph == 2:
                    sp.wait_ge(new_stored[s], half + 16)
            for s in range(2):
                load_nodes(s, s)
            in_pairs(sp, NC, node, PEEL)
        for s in range(2):
            sp.wait_ge(new_stored[s], half * 2 + 16)

    def gpsimd_program(pool):
        pool.memset(ones[:, :], 1.0).then_inc(prep, 1)
        pool.iota(iota_i[:, :], [[1, P]], base=0, channel_multiplier=0)
        pool.iota(head_base_i[:, :], [[1, 1]], base=-1, channel_multiplier=T)
        pool.wait_ge(prep, 1)
        pool.affine_select(out=ident[:, :], in_=ones[:, :], compare_op=ALU.is_equal, fill=0.0, base=0,
                           pattern=[[-1, P]], channel_multiplier=1)
        pool.affine_select(out=upper[:, :], in_=ones[:, :], compare_op=ALU.is_ge, fill=0.0, base=0,
                           pattern=[[1, P]], channel_multiplier=-1).then_inc(consts_made, 1)

        for ph in range(3):
            table = x_rows if ph == 0 else m_tab[ph - 1]
            if ph:
                for s in range(2):
                    pool.wait_ge(m_stored[s], 16 * (NC // 2) * ph + 16)

            def gather(i, s, b):
                pool.wait_ge(idx_loaded[s], i * 16 + (ph * 16 * (NB // 2) + 16))
                pool.wait_ge(step_done, b * G + (ph * T + G + 1))
                pool.sem_inc(turn_begun, 1)
                for g in range(steps_of(b)):
                    pool.indirect_dma_start(ring[:, s, g, :], None, table,
                                            bass.IndirectOffsetOnAxis(src_idx[:, s, g:g + 1], 0)
                                            ).then_inc(gathered[ph][s][g >= HALF], 16)

            in_pairs(pool, NB, gather, 1)

            for s in range(2):
                for h in range(2):
                    pool.wait_ge(run_stored[s][h], 16 * TURNS * (ph + 1) + 16)
            pool.wait_ge(tables_ready, 1)
            pool.wait_ge(zero_stored, 16)
            pool.indirect_dma_start(head_rows[:, :], None, states,
                                    bass.IndirectOffsetOnAxis(head_idx[:, 0:1], 0)).then_inc(head_got, 16)
            pool.wait_ge(head_ready, ph + 1)
            pool.indirect_dma_start(states, bass.IndirectOffsetOnAxis(head_idx[:, 0:1], 0),
                                    head_fixed[:, :], None).then_inc(head_put, 16)
            pool.wait_ge(head_put, 16 * (ph + 1))

            def node_gather(i, s, j):
                pool.wait_ge(end_ready, j + (ph * NC + 1))
                pool.wait_ge(aggT_copied, j + (ph * NC + 1))
                pool.sem_inc(turn_begun, 1)
                for c in range(size(j)):
                    pool.indirect_dma_start(agg[:, s, c, :], None, states,
                                            bass.IndirectOffsetOnAxis(end_slot[:, s, c:c + 1], 0)
                                            ).then_inc(agg_gathered[s], 16)

            in_pairs(pool, NC, node_gather, PEEL)

    def tensor_program(pe):
        pe.wait_ge(weights_loaded, 16 * 6)
        pe.wait_ge(tables_ready, 2)

        pe.wait_ge(consts_made, 1)
        pe.wait_ge(ends_ready, 1)
        for n in range(2):
            mm = nc.tensor.matmul(ps_ms[1][0:D, n * P:(n + 1) * P], ends_b[:, n, :], ident[:, :], start=True, stop=True)
        mm.then_inc(rows_ready, 1)

        def hidden(i, s, b, g):
            bank = (s * NG + g) % 2
            pe.wait_ge(h_copied, b * NG + (g + 1))
            nc.tensor.matmul(ps_h[bank][0:D, :], w1z_sb[:, g, :], ea_sb[:, s, :], start=True, stop=True
                             ).then_inc(h_ready, 1)

        def weight(i, s, b, g):
            bank = (s * NG + g) % 2
            pe.wait_ge(h_copied, b * NG + (g + 3))
            pe.wait_ge(msg_done, b * NG + (g + 1))
            for q in range(GQ):
                mm = nc.tensor.matmul(ps_w[bank][:, q * D:(q + 1) * D], hT[:, bank, q * P:(q + 1) * P],
                                      w2a_sb[:, :], start=True, stop=True)
            mm.then_inc(w_ready, 1)

        def edge(i, s, b):
            pe.wait_ge(ea_loaded[s], i * 16 + 16)
            groups = -(-steps_of(b) // GQ)
            hidden(i, s, b, 0)
            for g in range(1, groups):
                hidden(i, s, b, g)
                weight(i, s, b, g - 1)
            weight(i, s, b, groups - 1)
            pe.wait_ge(hot_ready, b + 1)
            for g in range(steps_of(b)):
                mm = nc.tensor.matmul(ps_hist[:, 0:NBLK], hot_lo[:, g, :], hot_hi[:, g, :],
                                      start=False, stop=False, skip_group_check=True)
            mm.then_inc(hist_added, 1)
            if s == 0:
                pe.wait_ge(xT_loaded, i * 16 + 16)
                pe.wait_ge(pre_copied, i + 1)
                for c in range(CS):
                    mm = nc.tensor.matmul(ps_pre[:, c * D:(c + 1) * D], xT_sb[:, c * P:(c + 1) * P], wsa_sb[:, :],
                                          start=True, stop=True)
                mm.then_inc(pre_ready, 1)

        nc.tensor.matmul(ps_hist[:, 0:NBLK], zeros_w[:, :], zeros_w[:, 0:NBLK], start=True, stop=False, skip_group_check=True)
        in_pairs(pe, NB, edge, 1)

        pe.wait_ge(hist_copied, 1)
        nc.tensor.matmul(ps_ms[1][:, 0:NBLK], upper[:, :], hist[:, :], start=True, stop=True)
        nc.tensor.matmul(ps_ms[1][:, P:P + NBLK], ones[:, :], hist[:, :], start=True, stop=True).then_inc(hist_summed, 1)

        for ph in range(3):
            pe.wait_ge(step_done, (ph + 1) * T + 2 * G + 1)
            pe.transpose(ps_t[0][0:D, 0:P], run[:, 1, GL - 1, :], ident[:, :]).then_inc(last_T, 1)
            pe.wait_ge(carry_ready, ph + 1)
            pe.transpose(ps_t[1][:, 0:D], carry_in[:, :], ident[0:D, 0:D]).then_inc(carry_back, 1)
            pe.wait_ge(head_ready, ph + 1)

            def agg_transposes(i, s, j):
                n = size(j)
                pe.wait_ge(agg_gathered[s], gathered_blocks(i, s, j) * 16 + (ph * sum(SIZES[s::2]) + n) * 16)
                if ph < 2:
                    pe.wait_ge(nodeT_copied, j + (ph * NC + 1))
                for c in range(n):
                    mm = pe.transpose(ps_t[c // 4][0:D, (c % 4) * P:(c % 4 + 1) * P], agg[:, s, c, :], ident[:, :])
                mm.then_inc(aggT_ready, 1)

            def agg_products(i, s, j):
                pe.wait_ge(aggT_copied, j + (ph * NC + 3))
                pe.wait_ge(o_used, j + (ph * NC + 1))
                for c in range(size(j)):
                    mm = nc.tensor.matmul(ps_o[c // 4][:, (c % 4) * D:(c % 4 + 1) * D], aggT[:, s, c * P:(c + 1) * P],
                                          wn_sb[:, ph, :], start=True, stop=True)
                mm.then_inc(o_ready, 1)

            def node_transposes(i, s, j):
                pe.wait_ge(node_ready, j + (ph * NC + 1))
                for c in range(size(j)):
                    mm = pe.transpose(ps_t[c // 4][0:D, (c % 4) * P:(c % 4 + 1) * P], node_new[:, s, c, :], ident[:, :])
                mm.then_inc(nodeT_ready, 1)

            def node_products(i, s, j):
                pe.wait_ge(nodeT_copied, j + (ph * NC + 3))
                pe.wait_ge(m_copied, j + (ph * NC + 1))
                pe.wait_ge(self_copied, j + (ph * NC + 1))
                for c in range(size(j)):
                    mm = nc.tensor.matmul(ps_ms[c // 2][:, (c % 2) * 2 * D:(c % 2 + 1) * 2 * D],
                                          nodeT[:, s, c * P:(c + 1) * P], wpsa_sb[:, ph, :], start=True, stop=True)
                mm.then_inc(ms_ready, 1)

            def both(i, s, j):
                ahead = not among_last(j, NC, 2)
                node_transposes(i, s, j)
                if ahead:
                    agg_transposes(i + 1, s, j + 2)
                node_products(i, s, j)
                if ahead:
                    agg_products(i + 1, s, j + 2)

            def agg_only(i, s, j):
                agg_transposes(i, s, j)
                agg_products(i, s, j)

            if ph < 2:
                for s in range(2):
                    agg_only(0, s, s)
                in_pairs(pe, NC, both, PEEL)
            else:
                in_pairs(pe, NC, agg_only, PEEL)

    def scalar_program(act):
        act.wait_ge(weights_loaded, 16 * 6)
        act.wait_ge(tables_ready, 2)

        def edge(i, s, b):
            for g in range(-(-steps_of(b) // GQ)):
                bank = (s * NG + g) % 2
                act.wait_ge(h_ready, b * NG + (g + 1))
                act.wait_ge(w_ready, b * NG + (g + 1))
                nc.scalar.activation(hT[0:D, bank, :], ps_h[bank][0:D, :], ACT.Relu, bias=b1_sb[:, 0:1]
                                     ).then_inc(h_copied, 1)
            if s == 0:
                act.wait_ge(pre_ready, i + 1)
                act.wait_ge(pre_stored, i * 16 + 16)
                nc.scalar.activation(flat(pre_sb[:, :, :]), ps_pre[:, 0:CS * D], ACT.Copy).then_inc(pre_copied, 1)

        in_pairs(act, NB, edge, 1)

        for ph in range(3):
            def root(count, j, eps):
                n = size(j)
                of = mean_var[:, 0:n, 1] if eps is eps_col else stat[:, 0, 0:n]
                act.wait_ge(var_in, count)
                nc.scalar.activation(stat[:, 1, 0:n], of, ACT.Sqrt, bias=eps[:, 0:1]).then_inc(std_ready, 1)

            def copy_blocks(to, n):
                for c0 in range(0, n, 4):
                    c1 = min(n, c0 + 4)
                    last = nc.scalar.activation(to[:, c0 * P:c1 * P], ps_t[c0 // 4][0:D, 0:(c1 - c0) * P], ACT.Copy)
                return last

            def copy_agg(i, s, j):
                act.wait_ge(aggT_ready, j + (ph * NC + 1))
                copy_blocks(aggT[:, s, :], size(j)).then_inc(aggT_copied, 1)
                if not among_last(j, NC, 2):
                    nc.scalar.activation(end_slot[:, s, :], end_idx[:, bass.ds(start(j + 2), C)], ACT.Copy
                                         ).then_inc(end_ready, 1)

            def copy_nodes(i, s, j):
                act.wait_ge(nodeT_ready, j + (ph * NC + 1))
                copy_blocks(nodeT[0:D, s, :], size(j)).then_inc(nodeT_copied, 1)

            def copy_products(i, s, j):
                act.wait_ge(ms_ready, j + (ph * NC + 1))
                act.wait_ge(m_stored[s], i * 16 + (ph * 16 * (NC // 2) + 16))
                n = size(j)
                banks = range(-(-n // 2))
                ms = [ps_ms[q][:, 0:min(2, n - 2 * q) * 2 * D].rearrange("p (w d) -> p w d", d=2 * D) for q in banks]
                for q in banks:
                    last = nc.scalar.activation(m_sb[:, s, 2 * q:min(2 * q + 2, n), :], ms[q][:, :, 0:D],
                                                ACT.Relu, bias=zero_col[:, 0:1])
                last.then_inc(m_copied, 1)
                act.wait_ge(self_stored[s], i * 16 + (ph * 16 * (NC // 2) + 16))
                for q in banks:
                    last = nc.scalar.activation(self_out[:, s, 2 * q:min(2 * q + 2, n), :], ms[q][:, :, D:2 * D], ACT.Copy)
                last.then_inc(self_copied, 1)

            if ph < 2:
                eps = eps_col if ph == 0 else zero_col

                def both(i, s, j):
                    copy_nodes(i, s, j)
                    if not among_last(j, NC, 2):
                        copy_agg(i + 1, s, j + 2)
                    if not among_last(j, NC, 1):
                        root(j + (ph * NC + 2), j + 1, eps)
                    copy_products(i, s, j)

                copy_agg(0, 0, 0)
                copy_agg(0, 1, 1)
                root(ph * NC + 1, 0, eps)
                in_pairs(act, NC, both, PEEL)
            else:
                def roots(i, s, j):
                    if not among_last(j, NC, 1):
                        copy_agg(i + s, 1 - s, j + 1)
                    root(j * 2 + (2 * NC + 1), j, zero_col)
                    root(j * 2 + (2 * NC + 2), j, eps_col)

                copy_agg(0, 0, 0)
                in_pairs(act, NC, roots, PEEL)

    def vector_program(dve):
        done = [0]

        def chain(ins):
            done[0] += 1
            ins.then_inc(end_step, 1)
            dve.wait_ge(end_step, done[0])

        v = nc.vector
        chain(v.memset(run[:, 1, G - 1, :], 0.0))
        v.memset(zrow[:, :], 0.0).then_inc(zero_ready, 1)
        v.memset(zeros_w[:, :], 0.0)
        v.memset(eps_col[:, :], LN_EPS)
        v.memset(zero_col[:, :], 0.0)
        v.memset(nodeT[D:D1, :, :], 1.0)
        v.memset(xT_sb[D:D + 2, :], 1.0)
        v.memset(carry[:, 0:1], 0.0)
        v.memset(cont_row[:, 0:1], 0.0)
        v.memset(keep[:, 0:1], 0.0)
        v.memset(end_idx[:, NBLK:], 0)
        v.memset(hT[D:D1, :, :], 1.0)
        v.memset(head_rows[:, 0:1], 0.0).then_inc(tables_ready, 2)

        dve.wait_ge(dst_loaded, 16)
        dve.wait_ge(consts_made, 1)
        v.tensor_copy(ends_f[:, 0:1], dst_i[:, 0:1])
        chain(v.tensor_copy(ends_f[:, 1:2], dst_i[:, T - 1:T]))
        v.tensor_scalar(ends_b[:, 0, :], ones[:, 0:D], ends_f[:, 0:1], None, ALU.mult)
        v.tensor_scalar(ends_b[:, 1, :], ones[:, 0:D], ends_f[:, 1:2], None, ALU.mult).then_inc(ends_ready, 1)
        v.tensor_tensor(keep[:, 1:T], dst_i[:, 1:T], dst_i[:, 0:T - 1], ALU.is_equal)
        v.tensor_scalar(dst_hi_i[:, :], dst_i[:, :], 7, None, ALU.arith_shift_right)
        chain(v.tensor_scalar(dst_lo_i[:, :], dst_i[:, :], P - 1, None, ALU.bitwise_and))
        v.tensor_copy(dst_hi[:, :], dst_hi_i[:, :])
        v.tensor_copy(dst_lo[:, :], dst_lo_i[:, :])
        v.tensor_copy(head_base[:, :], head_base_i[:, :])
        v.tensor_copy(iota[:, :], iota_i[:, :])
        chain(v.tensor_scalar(same_first[:, :], dst_i[:, :], ends_f[:, 0:1], None, ALU.is_equal))
        chain(v.tensor_reduce(head_n[:, :], same_first[:, :], AX.X, ALU.add))
        v.tensor_tensor(head_idx[:, :], head_n[:, :], head_base[:, :], ALU.add)
        dve.wait_ge(rows_ready, 1)
        chain(v.tensor_copy(last_row[:, :], ps_ms[1][0:D, P:2 * P]))
        v.tensor_tensor(cont_row[:, 1:P], ps_ms[1][0:D, 1:P], last_row[:, 0:P - 1], ALU.is_equal)
        chain(v.tensor_tensor(whole_row[:, :], ps_ms[1][0:D, 0:P], last_row[:, :], ALU.is_equal))
        chain(v.tensor_tensor(pass_row[:, :], whole_row[:, :], cont_row[:, :], ALU.mult))

        for ph in range(3):
            merge = ALU.add if ph == 0 else ALU.max

            def edge(i, s, b):
                steps = steps_of(b)
                dve.wait_ge(step_done, b * G + (ph * T + G + 1))
                v.tensor_scalar(keep_b[:, s, 0:steps], keep[:, bass.ds(b * G, steps)], 0.0, None, ALU.add).then_inc(keep_copied, 1)
                if ph == 0:
                    dve.wait_ge(hist_added, b + 1)
                    v.tensor_tensor(hot_hi[:, 0:steps, :], iota[:, 0:NBLK].unsqueeze(1).to_broadcast([P, steps, NBLK]),
                                    dst_hi[:, bass.ds(b * G, steps)].unsqueeze(2).to_broadcast([P, steps, NBLK]),
                                    ALU.is_equal)
                    v.tensor_tensor(hot_lo[:, 0:steps, :], iota[:, :].unsqueeze(1).to_broadcast([P, steps, P]),
                                    dst_lo[:, bass.ds(b * G, steps)].unsqueeze(2).to_broadcast([P, steps, P]), ALU.is_equal
                                    ).then_inc(hot_ready, 1)
                dve.wait_ge(keep_copied, b + (ph * NB + 1))
                for g in range(steps):
                    for h, (g0, g1) in enumerate(parts(steps)):
                        if g == g0:
                            full = parts(G)[h][1] - g0
                            dve.wait_ge(gathered[ph][s][h], i * (16 * full) + 16 * (g1 - g0))
                            dve.wait_ge(run_stored[s][h], i * 16 + (ph * 16 * TURNS + 16))
                    if ph == 0 and g % GQ == 0:
                        n, g_end = g // GQ, min(g + GQ, steps)
                        dve.wait_ge(w_ready, b * NG + (n + 3))
                        v.tensor_tensor(flat(ring[:, s, g:g_end]), ps_w[(s * NG + n) % 2][:, 0:(g_end - g) * D],
                                        flat(ring[:, s, g:g_end]), ALU.mult).then_inc(msg_done, 1)
                        dve.wait_ge(msg_done, b * NG + (n + 3))
                    before = run[:, s, g - 1, :] if g else run[:, 1 - s, G - 1, :]
                    dve.wait_ge(step_done, b * G + (ph * T + 2 * G + 1 + g))
                    v.scalar_tensor_tensor(run[:, s, g, :], before, keep_b[:, s, g:g + 1], ring[:, s, g, :],
                                           ALU.mult, merge).then_inc(step_done, 1)

            in_pairs(dve, NB, edge, 1)

            if ph == 0:
                dve.wait_ge(hist_added, NB + 1)
                v.tensor_copy(hist[:, :], ps_hist[:, 0:NBLK]).then_inc(hist_copied, 1)
            dve.wait_ge(last_T, ph + 1)
            v.tensor_tensor_scan(carry[:, 1:P + 1], pass_row[:, :], ps_t[0][0:D, 0:P], 0.0, ALU.mult, merge
                                 ).then_inc(carried, 1)
            dve.wait_ge(carried, ph + 1)
            v.tensor_tensor(carry_in[:, :], cont_row[:, :], carry[:, 0:P], ALU.mult).then_inc(carry_ready, 1)
            if ph == 0:
                dve.wait_ge(hist_summed, 1)
                chain(v.tensor_tensor_scan(nodes_cum[:, :], ones[:, 0:NBLK], ps_ms[1][:, P:P + NBLK], 0.0, ALU.mult, ALU.add))
                chain(v.tensor_tensor(end_a[:, :], nodes_cum[:, :], ps_ms[1][:, P:P + NBLK], ALU.subtract))
                chain(v.tensor_tensor(end_b[:, :], ps_ms[1][:, 0:NBLK], end_a[:, :], ALU.add))
                v.tensor_scalar(end_a[:, :], end_b[:, :], -float(ZROW + 1), None, ALU.add)
                chain(v.tensor_scalar(some[:, :], hist[:, :], 0.0, None, ALU.is_gt))
                chain(v.tensor_tensor(end_b[:, :], end_a[:, :], some[:, :], ALU.mult))
                chain(v.tensor_scalar(end_idx[:, 0:NBLK], end_b[:, :], float(ZROW), None, ALU.add))
            for s in range(2):
                v.tensor_copy(end_slot[:, s, :], end_idx[:, s * C:(s + 1) * C]).then_inc(end_ready, 1)
            dve.wait_ge(head_got, 16 * (ph + 1))
            dve.wait_ge(carry_back, ph + 1)
            v.tensor_tensor(head_fixed[:, :], ps_t[1][:, 0:D], head_rows[:, :], merge).then_inc(head_ready, 1)

            n_in = 32 if ph != 1 else 16
            base_in = [0, 32 * (NC // 2), 48 * (NC // 2)][ph]
            n_steps = [4, 5, 7][ph]
            base_steps = [0, 4 * NC, 9 * NC][ph]

            def node(i, s, j):
                at, n = [0], size(j)

                def link(ins):
                    at[0] += 1
                    ins.then_inc(node_step, 1)
                    dve.wait_ge(node_step, j * n_steps + (base_steps + at[0]))

                def wide(k):
                    return stat[:, k, 0:n].unsqueeze(2).to_broadcast([P, n, D])

                def layer_norm(out_ap, count):
                    for c in range(n):
                        last = v.bn_stats(bn[:, c, :], t1[:, c, :])
                    link(last)
                    v.memset(scratch[:, 1:2], 0.0)
                    for c in range(n):
                        last = v.bn_aggr(mean_var[:, c, :], bn[:, c, :])
                    last.then_inc(var_in, 1)
                    dve.wait_ge(std_ready, count)
                    link(v.reciprocal(stat[:, 2, 0:n], stat[:, 1, 0:n]))
                    for c in range(n):
                        last = v.tensor_scalar(out_ap[:, c, :], t1[:, c, :], mean_var[:, c, 0:1], stat[:, 2, c:c + 1],
                                               ALU.subtract, ALU.mult)
                    last.then_inc(node_ready, 1)

                def l2_scale(count):
                    link(v.tensor_tensor(sq[:, 0:n, :], t2[:, 0:n, :], t2[:, 0:n, :], ALU.mult))
                    v.tensor_reduce(stat[:, 0, 0:n], sq[:, 0:n, :], AX.X, ALU.add).then_inc(var_in, 1)
                    dve.wait_ge(std_ready, count)
                    link(v.tensor_scalar(stat[:, 0, 0:n], stat[:, 1, 0:n], L2_EPS, None, ALU.max))
                    link(v.reciprocal(stat[:, 2, 0:n], stat[:, 0, 0:n]))

                dve.wait_ge(o_ready, j + (ph * NC + 1))
                dve.wait_ge(node_in[s], i * n_in + (base_in + n_in))
                before = t2 if ph == 2 else t1
                for c0 in range(0, n, 4):
                    c1 = min(n, c0 + 4)
                    last = v.tensor_tensor(flat(before[:, c0:c1]), ps_o[c0 // 4][:, 0:(c1 - c0) * D],
                                           flat(self_in[:, s, c0:c1]), ALU.add)
                link(last)
                v.memset(scratch[:, 0:1], 0.0).then_inc(o_used, 1)
                if ph == 0:
                    link(v.scalar_tensor_tensor(t1[:, 0:n, :], t1[:, 0:n, :], 0.0, res_in[:, s, 0:n], ALU.max, ALU.add))
                    dve.wait_ge(new_stored[s], i * 16 + 16)
                    layer_norm(node_new[:, s], j + 1)
                elif ph == 1:
                    link(v.tensor_scalar(t2[:, 0:n, :], t1[:, 0:n, :], 0.0, None, ALU.max))
                    l2_scale(j + (NC + 1))
                    v.tensor_tensor(node_new[:, s, 0:n], t2[:, 0:n, :], wide(2), ALU.mult).then_inc(node_ready, 1)
                else:
                    l2_scale(j * 2 + (2 * NC + 1))
                    for c in range(n):
                        last = v.scalar_tensor_tensor(t1[:, c, :], t2[:, c, :], stat[:, 2, c:c + 1], res_in[:, s, c, :],
                                                      ALU.mult, ALU.add)
                    link(last)
                    dve.wait_ge(new_stored[s], i * 16 + (16 * (NC // 2) + 16))
                    layer_norm(node_new[:, s], j * 2 + (2 * NC + 2))
                assert at[0] == n_steps
                dve.wait_ge(node_ready, j + (ph * NC + 1))

            in_pairs(dve, NC, node, PEEL)

    return sync_program, gpsimd_program, tensor_program, scalar_program, vector_program


BG = 14
BE = P * BG
BNB = -(-E // BE)
BGL = -(-(E - (BNB - 1) * BE) // P)
BEP = (BNB - 1) * BE + P * BGL
B_STEPS = (BNB - 1) * (BG - 1) + BGL - 1
K = 8
BT = BNB // K
assert BT * K == BNB
SLOTS = 4
B_NG = -(-BG // GQ)
B_PART = 8
assert B_PART % GQ == 0 and B_PART < BGL and B_NG * ED <= P
B_SIZES = [C] * (BT - 1) + [4, 3]
BNC = len(B_SIZES)
B_DONE = BNB - 4
assert sum(B_SIZES) == NBLK
K_SUMS, K_PRODUCTS = 3, 4
AGG_ROWS = NP + P


def b_steps(b):
    return BGL if isinstance(b, int) and b == BNB - 1 else BG


def b_groups(b):
    return -(-b_steps(b) // GQ)


def b_gathers(J, k, b, h):
    n = B_PART if h == 0 else BG - B_PART
    missing = BG - b_steps(b) if h == 1 else 0
    return J * (16 * n * (K // SLOTS)) + 16 * (n * (k // SLOTS + 1) - missing)


def b_size(j):
    return B_SIZES[j] if isinstance(j, int) else C


def b_blocks(j, per):
    return bass.ds((sum(B_SIZES[:j]) if isinstance(j, int) else j * C) * per, b_size(j) * per)


def build_by_batch(nc, ctx, bounds_f, bounds_i, bounds_ready, src, dst, nxt, prv, ea, x_rows, x_pm, xT, w1z, b1,
                   w2a, wsa, wn, wpsa, out):
    def sb(name, shape, dt=F32):
        return ctx.enter_context(nc.sbuf_tensor("b_" + name, shape, dt))

    def sem(name):
        return ctx.enter_context(nc.semaphore(name))

    def sem2(name):
        return [sem(f"{name}{s}") for s in range(2)]

    agg_tab = [nc.dram_tensor(f"b_agg_tab{i}", (AGG_ROWS, D), F32).ap() for i in range(3)]
    agg_tab_v = [t[0:NP, :].rearrange("(k p) d -> p k d", p=P) for t in agg_tab]
    m_tab = [nc.dram_tensor(f"b_m_tab{i}", (NP, D), F32).ap() for i in range(2)]
    m_tab_v = [m.rearrange("(k p) d -> p k d", p=P) for m in m_tab]
    self_tab = [nc.dram_tensor(f"b_self_tab{i}", (P, NBLK * D), F32).ap() for i in range(2)]
    x1_tab = nc.dram_tensor("b_x1_tab", (P, NBLK * D), F32).ap()

    src_idx = sb("src_idx", [P, SLOTS, BG], I32)
    ring = sb("ring", [P, SLOTS, BG, D])
    dst_i = sb("dst_i", [P, BNB, BG], I32)
    nxt_i = sb("nxt_i", [P, BNB, BG], I32)
    prv_i = sb("prv_i", [P, BNB, BG], I32)
    rel = sb("rel", [P, BNB, BG])
    end_rel = sb("end_rel", [P, BNB, BG])
    is_end = sb("is_end", [P, BNB, BG])
    keep = sb("keep", [P, BNB, BG])
    head_ends = sb("head_ends", [P, BNB])
    cont_rel = sb("cont_rel", [P, BNB])
    head_rel = sb("head_rel", [P, BNB])
    whole = sb("whole", [P, BNB])
    passes = sb("passes", [P, BNB])
    keep_b = sb("keep_b", [P, 2, BG])
    iota_i = sb("iota_i", [P, P], I32)
    iota1 = sb("iota1", [P, P])
    hot = sb("hot", [P, 2, BG, P])
    hot_head = sb("hot_head", [P, 2, P])
    pass_bc = sb("pass_bc", [P, 2, D])
    pass_row = sb("pass_row", [D, P])
    held = sb("held", [D, 2, P + 1])
    held_in = sb("held_in", [P, D])
    head_add = sb("head_add", [P, D])
    rows_out = sb("rows_out", [P, 2, D])
    ea_sb = sb("ea_sb", [B_NG * ED, 2, GQ * P])
    hT = sb("hT", [D1, 2, GQ * P])
    w_sb = sb("w_sb", [P, 2, BG * D])
    w1z_sb = sb("w1z_sb", [B_NG * ED, B_NG, D])
    b1_sb = sb("b1_sb", [D, 1])
    w2a_sb = sb("w2a_sb", [D1, D])
    ident = sb("ident", [P, P])
    ones = sb("ones", [P, P])
    agg = sb("agg", [P, C, D])
    aggT = sb("aggT", [D, C * P])
    self_in = sb("self_in", [P, C, D])
    res_in = sb("res_in", [P, C, D])
    xT_sb = sb("xT_sb", [D + 2, C * P])
    t1 = sb("t1", [P, C, D])
    t2 = sb("t2", [P, C, D])
    sq = sb("sq", [P, C, D])
    stat = sb("stat", [P, 3, C])
    bn = sb("bn", [P, C, 6])
    mean_var = sb("mean_var", [P, C, 2])
    scratch = sb("scratch", [P, 2])
    node_new = sb("node_new", [P, C, D])
    nodeT = sb("nodeT", [D1, C * P])
    m_sb = sb("m_sb", [P, C, D])
    self_out = sb("self_out", [P, C, D])
    wsa_sb = sb("wsa_sb", [D + 2, D])
    wn_sb = sb("wn_sb", [D, 3, D])
    wpsa_sb = sb("wpsa_sb", [D1, 2, 2 * D])
    eps_col = sb("eps_col", [P, 1])
    zero_col = sb("zero_col", [P, 1])
    zero_rows = sb("zero_rows", [P, D])

    ps = [ctx.enter_context(nc.psum_tensor(f"b_ps{i}", [P, 512], F32)) for i in range(8)]
    ps_h, ps_w, ps_last, ps_row, ps_agg, ps_head = ps[0:2], ps[2:4], ps[4], ps[5], ps[6], ps[7]
    ps_t, ps_o, ps_ms = ps[0:2], ps[2:4], ps[0:4]

    idx_loaded = [sem(f"b_idx_loaded{s}") for s in range(SLOTS)]
    tables_loaded, weights_loaded = sem("b_tables_loaded"), sem("b_weights_loaded")
    ea_loaded = sem2("b_ea_loaded")
    gathered = [[[sem(f"b_gathered{ph}_{s}_{h}") for h in range(2)] for s in range(SLOTS)] for ph in range(3)]
    turn_begun, load_begun, store_begun = sem("b_turn_begun"), sem("b_load_begun"), sem("b_store_begun")
    prep, consts_made, consts_set, spread, table_step = (sem("b_prep"), sem("b_consts_made"), sem("b_consts_set"),
                                                         sem("b_spread"), sem("b_table_step"))
    h_ready, h_copied, w_ready, w_copied = sem("b_h_ready"), sem("b_h_copied"), sem("b_w_ready"), sem("b_w_copied")
    msg_done = sem("b_msg_done")
    hot_ready, keep_copied = sem("b_hot_ready"), sem("b_keep_copied")
    step_done = sem("b_step_done")
    last_T, scanned, held_T, held_copied = sem("b_last_T"), sem("b_scanned"), sem("b_held_T"), sem("b_held_copied")
    held_moved = sem("b_held_moved")
    row_ready, row_copied = sem("b_row_ready"), sem("b_row_copied")
    head_ready, head_copied = sem("b_head_ready"), sem("b_head_copied")
    extracted = sem("b_extracted")
    rows_ready, rows_stored = sem("b_rows_ready"), sem("b_rows_stored")
    zeros_stored = sem("b_zeros_stored")
    node_in = sem("b_node_in")
    aggT_ready, aggT_copied, o_ready, o_used = sem("b_aggT_ready"), sem("b_aggT_copied"), sem("b_o_ready"), sem("b_o_used")
    node_step, node_ready, var_in, std_ready = sem("b_node_step"), sem("b_node_ready"), sem("b_var_in"), sem("b_std_ready")
    nodeT_ready, nodeT_copied = sem("b_nodeT_ready"), sem("b_nodeT_copied")
    ms_ready, m_copied, self_copied = sem("b_ms_ready"), sem("b_m_copied"), sem("b_self_copied")
    m_stored, self_stored, new_stored = sem("b_m_stored"), sem("b_self_stored"), sem("b_new_stored")

    def flat(ap):
        return ap.rearrange("p c d -> p (c d)")

    def turns(eng, body, tail):
        for k in range(K):
            body(0, k, k)
        with eng.Fori(1, BT - 1) as J:
            for k in range(K):
                body(J, k, J * K + k)
        for k in range(K):
            body(BT - 1, k, (BT - 1) * K + k)
        tail()

    def is_int(v, at):
        return isinstance(v, int) and v == at

    def sync_program(sp):
        sp.sem_inc(h_copied, 2)
        sp.sem_inc(w_copied, 2)
        sp.sem_inc(step_done, 1)
        sp.sem_inc(extracted, SLOTS)
        sp.sem_inc(rows_ready, 1)
        sp.sem_inc(rows_stored, 32)
        for stored in (m_stored, self_stored, new_stored):
            sp.sem_inc(stored, 16)
        for s in range(SLOTS):
            sp.dma_start(src_idx[:, s, :], src[:, s * BG:(s + 1) * BG]).then_inc(idx_loaded[s], 16)
        for to, of in [(dst_i, dst), (nxt_i, nxt), (prv_i, prv)]:
            sp.dma_start(flat(to[:, :, :]), of).then_inc(tables_loaded, 16)
        for to, of in [(w1z_sb[:, :, :], w1z[0:B_NG * ED, 0:B_NG, :]), (b1_sb[:, :], b1), (w2a_sb[:, :], w2a),
                       (wn_sb[:, :, :], wn), (wpsa_sb[:, :, :], wpsa), (wsa_sb[:, :], wsa)]:
            sp.dma_start(to, of).then_inc(weights_loaded, 16)
        for s in range(2):
            sp.dma_start(ea_sb[:, s, :], ea[:, s, :]).then_inc(ea_loaded[s], 16)
        sp.wait_ge(consts_set, 1)
        for ph in range(3):
            sp.dma_start(agg_tab[ph][NP - P:NP, :], zero_rows[:, :]).then_inc(zeros_stored, 16)
        sp.wait_ge(zeros_stored, 48)

        for ph in range(3):
            base, node_base = ph * BNB, ph * BNC

            def store_rows(b):
                row = sp.value_load(bounds_i[0:1, bass.ds(b, 1)], min_val=0, max_val=N)
                sp.wait_ge(rows_ready, b + (base + 2))
                sp.wait_ge(rows_stored, b * 16 + (base * 16 + 32))
                sp.sem_inc(store_begun, 1)
                return row

            def load_sums(j):
                sp.dma_start(agg[:, 0:b_size(j), :], agg_tab_v[ph][:, b_blocks(j, 1), :]).then_inc(node_in, 16)

            def load_nodes(j):
                n, cols = b_size(j), b_blocks(j, D)
                if ph == 0:
                    sp.dma_start(xT_sb[0:D, 0:n * P], xT[:, b_blocks(j, P)]).then_inc(node_in, 16)
                else:
                    sp.dma_start(flat(self_in[:, 0:n, :]), self_tab[ph - 1][:, cols]).then_inc(node_in, 16)
                if ph != 1:
                    sp.dma_start(flat(res_in[:, 0:n, :]), (x_pm if ph == 0 else x1_tab)[:, cols]).then_inc(node_in, 16)

            def store_nodes(j):
                n, cols = b_size(j), b_blocks(j, D)
                sp.wait_ge(node_ready, j + (node_base + 1))
                if ph != 1:
                    sp.dma_start((x1_tab if ph == 0 else out)[:, cols], flat(node_new[:, 0:n, :])).then_inc(new_stored, 16)
                if ph < 2:
                    sp.wait_ge(m_copied, j + (node_base + 1))
                    sp.dma_start(m_tab_v[ph][:, b_blocks(j, 1), :], m_sb[:, 0:n, :]).then_inc(m_stored, 16)
                    sp.wait_ge(self_copied, j + (node_base + 1))
                    sp.dma_start(self_tab[ph][:, cols], flat(self_out[:, 0:n, :])).then_inc(self_stored, 16)

            def body(J, k, b):
                s = k % SLOTS
                if not (ph == 2 and isinstance(J, int) and J == BT - 1 and k >= K - SLOTS):
                    for h in range(2):
                        sp.wait_ge(gathered[ph][s][h], b_gathers(J, k, b, h))
                        sp.sem_inc(load_begun, 1)
                    ahead = k - (K - SLOTS) if is_int(J, BT - 1) and k >= K - SLOTS else b + SLOTS
                    sp.dma_start(src_idx[:, s, :], src[:, bass.ds(ahead * BG, BG)]).then_inc(idx_loaded[s], 16)
                if ph == 0 and not (is_int(J, BT - 1) and k >= K - 2):
                    sp.wait_ge(w_ready, b * B_NG + B_NG)
                    sp.dma_start(ea_sb[:, k % 2, :], ea[:, bass.ds(b + 2, 1), :].rearrange("a b c -> a (b c)")
                                 ).then_inc(ea_loaded[k % 2], 16)
                if not is_int(b, 0):
                    row = store_rows(b - 1)
                    sp.dma_start(agg_tab[ph][bass.ds(row, P), :], rows_out[:, (k - 1) % 2, :]).then_inc(rows_stored, 16)
                if not is_int(J, 0):
                    if k == 2:
                        load_nodes(J - 1)
                        load_sums(J - 1)
                    if k == K_PRODUCTS + 1:
                        store_nodes(J - 1)
                if is_int(b, B_DONE + 2):
                    load_nodes(BNC - 2)
                    load_sums(BNC - 2)

            def tail():
                row = store_rows(BNB - 1)
                sp.dma_start(agg_tab[ph][bass.ds(row, P), :], rows_out[:, 1, :]).then_inc(rows_stored, 16)
                sp.wait_ge(node_ready, node_base + BNC - 1)
                load_nodes(BNC - 1)
                sp.wait_ge(rows_stored, (base + BNB) * 16 + 32)
                load_sums(BNC - 1)
                store_nodes(BNC - 2)
                store_nodes(BNC - 1)
                if ph < 2:
                    sp.wait_ge(self_stored, 16 * (node_base + BNC) + 16)
                if ph != 1:
                    sp.wait_ge(new_stored, 16 * BNC * (1 if ph == 0 else 2) + 16)

            turns(sp, body, tail)

    def gpsimd_program(pool):
        pool.memset(ones[:, :], 1.0).then_inc(prep, 1)
        pool.iota(iota_i[:, :], [[1, P]], base=1, channel_multiplier=0)
        pool.wait_ge(prep, 1)
        pool.affine_select(out=ident[:, :], in_=ones[:, :], compare_op=ALU.is_equal, fill=0.0, base=0,
                           pattern=[[-1, P]], channel_multiplier=1).then_inc(consts_made, 1)
        for ph in range(3):
            table = x_rows if ph == 0 else m_tab[ph - 1]
            if ph:
                pool.wait_ge(m_stored, 16 * BNC * ph + 16)

            def body(J, k, b):
                s = k % SLOTS
                pool.wait_ge(idx_loaded[s], J * (16 * (K // SLOTS)) + 16 * (ph * BNB // SLOTS + k // SLOTS + 1))
                pool.wait_ge(extracted, b + (ph * BNB + 1))
                pool.sem_inc(turn_begun, 1)
                for g in range(b_steps(b)):
                    pool.indirect_dma_start(ring[:, s, g, :], None, table,
                                            bass.IndirectOffsetOnAxis(src_idx[:, s, g:g + 1], 0)
                                            ).then_inc(gathered[ph][s][g >= B_PART], 16)

            turns(pool, body, lambda: None)

    def tensor_program(pe):
        pe.wait_ge(weights_loaded, 16 * 6)
        pe.wait_ge(consts_set, 1)
        pe.wait_ge(consts_made, 1)
        pe.wait_ge(bounds_ready, 1)
        nc.tensor.matmul(ps_agg[:, 0:BNB], ones[0:1, :], bounds_f[0:1, 0:BNB], start=True, stop=True).then_inc(spread, 1)

        for ph in range(3):
            base, node_base = ph * BNB, ph * BNC

            def hidden(k, b, g):
                cols = min(GQ, b_steps(b) - g * GQ) * P
                pe.wait_ge(h_copied, b * B_NG + (g + 1))
                nc.tensor.matmul(ps_h[g % 2][0:D, 0:cols], w1z_sb[:, g, :], ea_sb[:, k % 2, 0:cols], start=True, stop=True
                                 ).then_inc(h_ready, 1)

            def weight(b, g):
                pe.wait_ge(h_copied, b * B_NG + (g + 3))
                pe.wait_ge(w_copied, b * B_NG + (g + 1))
                for q in range(min(GQ, b_steps(b) - g * GQ)):
                    mm = nc.tensor.matmul(ps_w[g % 2][:, q * D:(q + 1) * D], hT[:, g % 2, q * P:(q + 1) * P],
                                          w2a_sb[:, :], start=True, stop=True)
                mm.then_inc(w_ready, 1)

            def network(J, k, b):
                pe.wait_ge(ea_loaded[k % 2], J * (16 * K // 2) + 16 * (k // 2 + 1))
                hidden(k, b, 0)
                for g in range(1, b_groups(b)):
                    hidden(k, b, g)
                    weight(b, g - 1)
                weight(b, b_groups(b) - 1)

            def extract(b, q, s, g0, g1):
                if g0 == 0:
                    pe.wait_ge(rows_ready, b + (base + 1))
                    pe.wait_ge(step_done, b * (BG - 1) + (ph * B_STEPS + g1))
                for g in range(g0, g1):
                    mm = nc.tensor.matmul(ps_agg[:, 0:D], hot[:, q, g, :], ring[:, s, g, :], start=g == 0,
                                          stop=g == b_steps(b) - 1)
                if g1 == b_steps(b):
                    mm.then_inc(extracted, 1)

            def hand_on(b, q):
                pe.wait_ge(scanned, b + (base + 1))
                pe.transpose(ps_row[:, 0:D], held[:, q, 0:P], ident[0:D, 0:D]).then_inc(held_T, 1)

            def heads(b, q):
                pe.wait_ge(held_copied, b + (base + 1))
                nc.tensor.matmul(ps_head[:, 0:D], hot_head[:, q, :], held_in[:, :], start=True, stop=True).then_inc(head_ready, 1)

            def node_sums(j):
                pe.wait_ge(node_in, n_in * 16 * (j + 1) + base_in * 16)
                for c in range(b_size(j)):
                    mm = pe.transpose(ps_t[c // 4][0:D, (c % 4) * P:(c % 4 + 1) * P], agg[:, c, :], ident[:, :])
                mm.then_inc(aggT_ready, 1)
                pe.wait_ge(aggT_copied, j + (node_base + 1))
                for c in range(b_size(j)):
                    to = ps_o[c // 4][:, (c % 4) * D:(c % 4 + 1) * D]
                    mm = nc.tensor.matmul(to, aggT[:, c * P:(c + 1) * P], wn_sb[:, ph, :], start=True, stop=ph > 0)
                    if ph == 0:
                        mm = nc.tensor.matmul(to, xT_sb[:, c * P:(c + 1) * P], wsa_sb[:, :], start=False, stop=True)
                mm.then_inc(o_ready, 1)

            def node_products(j):
                pe.wait_ge(node_ready, j + (node_base + 1))
                for c in range(b_size(j)):
                    mm = pe.transpose(ps_t[c // 4][0:D, (c % 4) * P:(c % 4 + 1) * P], node_new[:, c, :], ident[:, :])
                mm.then_inc(nodeT_ready, 1)
                pe.wait_ge(nodeT_copied, j + (node_base + 1))
                for c in range(b_size(j)):
                    mm = nc.tensor.matmul(ps_ms[c // 2][:, (c % 2) * 2 * D:(c % 2 + 1) * 2 * D],
                                          nodeT[:, c * P:(c + 1) * P], wpsa_sb[:, ph, :], start=True, stop=True)
                mm.then_inc(ms_ready, 1)

            n_in, base_in = [(3, 0), (2, 3 * BNC), (3, 5 * BNC)][ph]

            def body(J, k, b):
                q, s = k % 2, k % SLOTS
                later = not is_int(J, 0)
                last = is_int(b, BNB - 1)
                if not is_int(b, 0):
                    hand_on(b - 1, 1 - q)
                pe.wait_ge(hot_ready, b + (base + 1))
                nc.tensor.matmul(ps_last[0:D, P:2 * P], pass_bc[:, q, :], ident[:, :], start=True, stop=True).then_inc(row_ready, 1)
                if not is_int(b, 0):
                    heads(b - 1, 1 - q)
                if later and k == K_SUMS + 1:
                    pe.wait_ge(o_used, J + node_base)
                if later and k == K_PRODUCTS + 1 and ph < 2:
                    pe.wait_ge(m_copied, J + node_base)
                    pe.wait_ge(self_copied, J + node_base)
                if ph == 0 and not last:
                    network(J, k + 1, b + 1)
                if last:
                    if ph == 0:
                        pe.wait_ge(w_copied, (BNB - 1) * B_NG + b_groups(b) + 2)
                    node_sums(BNC - 2)
                    extract(b, q, s, 0, B_PART)
                pe.wait_ge(step_done, b * (BG - 1) + (ph * B_STEPS + b_steps(b)))
                pe.wait_ge(row_copied, b + (base + 1))
                pe.transpose(ps_last[0:D, 0:P], ring[:, s, b_steps(b) - 1, :], ident[:, :]).then_inc(last_T, 1)
                if last:
                    hand_on(b, q)
                extract(b, q, s, B_PART if last else 0, b_steps(b))
                if later and k in (K_SUMS, K_PRODUCTS) and ph == 0:
                    pe.wait_ge(w_copied, b * B_NG + (2 * B_NG + 2))
                if later and k == K_SUMS:
                    node_sums(J - 1)
                if later and k == K_PRODUCTS and ph < 2:
                    node_products(J - 1)

            def tail():
                heads(BNB - 1, 1)
                if ph < 2:
                    node_products(BNC - 2)
                    pe.wait_ge(m_copied, BNC - 1 + node_base)
                    pe.wait_ge(self_copied, BNC - 1 + node_base)
                else:
                    pe.wait_ge(o_used, BNC - 1 + node_base)
                node_sums(BNC - 1)
                if ph < 2:
                    node_products(BNC - 1)
                    pe.wait_ge(m_copied, BNC + node_base)
                    pe.wait_ge(self_copied, BNC + node_base)

            if ph == 0:
                network(0, 0, 0)
            turns(pe, body, tail)

    def scalar_program(act):
        act.wait_ge(weights_loaded, 16 * 6)
        act.wait_ge(consts_set, 1)
        for ph in range(3):
            base, node_base = ph * BNB, ph * BNC

            def root(count, n, of, eps):
                act.wait_ge(var_in, count)
                nc.scalar.activation(stat[:, 1, 0:n], of, ACT.Sqrt, bias=eps[:, 0:1]).then_inc(std_ready, 1)

            def copy_blocks(to, n):
                for c0 in range(0, n, 4):
                    c1 = min(n, c0 + 4)
                    last = nc.scalar.activation(to[:, c0 * P:c1 * P], ps_t[c0 // 4][0:D, 0:(c1 - c0) * P], ACT.Copy)
                return last

            def node_sums(j):
                act.wait_ge(aggT_ready, j + (node_base + 1))
                copy_blocks(aggT[:, :], b_size(j)).then_inc(aggT_copied, 1)

            def node_roots(j):
                n = b_size(j)
                variances, squares = (n, mean_var[:, 0:n, 1], eps_col), (n, stat[:, 0, 0:n], zero_col)
                if ph == 0:
                    root(j + 1, *variances)
                elif ph == 1:
                    root(j + (BNC + 1), *squares)
                else:
                    root(j * 2 + (2 * BNC + 1), *squares)
                    root(j * 2 + (2 * BNC + 2), *variances)

            def node_products(j):
                act.wait_ge(nodeT_ready, j + (node_base + 1))
                n = b_size(j)
                banks = range(-(-n // 2))
                copy_blocks(nodeT[0:D, :], n).then_inc(nodeT_copied, 1)
                act.wait_ge(ms_ready, j + (node_base + 1))
                ms = [ps_ms[q][:, 0:min(2, n - 2 * q) * 2 * D].rearrange("p (w d) -> p w d", d=2 * D) for q in banks]
                act.wait_ge(m_stored, j * 16 + (node_base * 16 + 16))
                for q in banks:
                    last = nc.scalar.activation(m_sb[:, 2 * q:min(2 * q + 2, n), :], ms[q][:, :, 0:D],
                                                ACT.Relu, bias=zero_col[:, 0:1])
                last.then_inc(m_copied, 1)
                act.wait_ge(self_stored, j * 16 + (node_base * 16 + 16))
                for q in banks:
                    last = nc.scalar.activation(self_out[:, 2 * q:min(2 * q + 2, n), :], ms[q][:, :, D:2 * D], ACT.Copy)
                last.then_inc(self_copied, 1)

            def relu(b, g):
                cols = min(GQ, b_steps(b) - g * GQ) * P
                act.wait_ge(h_ready, b * B_NG + (g + 1))
                if not (is_int(b, 0) and g < 2):
                    act.wait_ge(w_ready, b * B_NG + (g - 1))
                nc.scalar.activation(hT[0:D, g % 2, 0:cols], ps_h[g % 2][0:D, 0:cols], ACT.Relu, bias=b1_sb[:, 0:1]
                                     ).then_inc(h_copied, 1)

            def copy_weights(b, q, g):
                cols = min(GQ, b_steps(b) - g * GQ) * D
                act.wait_ge(w_ready, b * B_NG + (g + 1))
                if g == 0 and not (is_int(b, 0) or is_int(b, 1)):
                    act.wait_ge(msg_done, b * 2 - 2)
                nc.scalar.activation(w_sb[:, q, g * GQ * D:g * GQ * D + cols], ps_w[g % 2][:, 0:cols], ACT.Copy).then_inc(w_copied, 1)

            def network(b, q):
                relu(b, 0)
                for g in range(1, b_groups(b)):
                    relu(b, g)
                    copy_weights(b, q, g - 1)
                copy_weights(b, q, b_groups(b) - 1)

            def copy_held(b):
                act.wait_ge(held_T, b + (base + 1))
                nc.scalar.activation(held_in[:, :], ps_row[:, 0:D], ACT.Copy).then_inc(held_copied, 1)

            def copy_heads(b):
                act.wait_ge(head_ready, b + (base + 1))
                nc.scalar.activation(head_add[:, :], ps_head[:, 0:D], ACT.Copy).then_inc(head_copied, 1)

            def body(J, k, b):
                if not is_int(b, 0):
                    copy_held(b - 1)
                act.wait_ge(row_ready, b + (base + 1))
                nc.scalar.activation(pass_row[:, :], ps_last[0:D, P:2 * P], ACT.Copy).then_inc(row_copied, 1)
                if not is_int(b, 0):
                    copy_heads(b - 1)
                if not is_int(J, 0) and k == K_SUMS + 1:
                    node_roots(J - 1)
                if ph == 0 and not is_int(b, BNB - 1):
                    network(b + 1, (k + 1) % 2)
                if is_int(b, BNB - 1):
                    node_sums(BNC - 2)
                    node_roots(BNC - 2)
                if not is_int(J, 0):
                    if k == K_SUMS:
                        node_sums(J - 1)
                    if k == K_PRODUCTS and ph < 2:
                        node_products(J - 1)

            def tail():
                copy_held(BNB - 1)
                copy_heads(BNB - 1)
                if ph < 2:
                    node_products(BNC - 2)
                node_sums(BNC - 1)
                node_roots(BNC - 1)
                if ph < 2:
                    node_products(BNC - 1)

            if ph == 0:
                network(0, 0)
            turns(act, body, tail)

    def vector_program(dve):
        v = nc.vector
        done = [0]

        def chain(ins):
            done[0] += 1
            ins.then_inc(table_step, 1)
            dve.wait_ge(table_step, done[0])

        v.memset(zero_rows[:, :], 0.0)
        v.memset(eps_col[:, :], LN_EPS)
        v.memset(zero_col[:, :], 0.0)
        v.memset(nodeT[D:D1, :], 1.0)
        v.memset(xT_sb[D:D + 2, :], 1.0)
        v.memset(hT[D:D1, :, :], 1.0).then_inc(consts_set, 1)
        dve.wait_ge(tables_loaded, 48)
        dve.wait_ge(consts_made, 1)
        dve.wait_ge(spread, 1)
        v.tensor_copy(iota1[:, :], iota_i[:, :])
        v.tensor_tensor(keep[:, :, :], dst_i[:, :, :], prv_i[:, :, :], ALU.is_equal)
        v.tensor_tensor(is_end[:, :, :], dst_i[:, :, :], nxt_i[:, :, :], ALU.not_equal)
        v.tensor_tensor(head_ends[:, :], dst_i[:, :, 0], nxt_i[:, :, BG - 1], ALU.not_equal)
        v.tensor_tensor(whole[:, :], dst_i[:, :, 0], dst_i[:, :, BG - 1], ALU.is_equal)
        chain(v.tensor_scalar(end_rel[:, :, :], dst_i[:, :, :], 1.0, None, ALU.add))
        chain(v.tensor_tensor(rel[:, :, :], end_rel[:, :, :], ps_agg[:, 0:BNB].unsqueeze(2).to_broadcast([P, BNB, BG]),
                              ALU.subtract))
        v.tensor_tensor(passes[:, :], whole[:, :], keep[:, :, 0], ALU.mult)
        v.tensor_tensor(end_rel[:, :, :], rel[:, :, :], is_end[:, :, :], ALU.mult)
        chain(v.tensor_tensor(cont_rel[:, :], rel[:, :, 0], keep[:, :, 0], ALU.mult))
        chain(v.tensor_tensor(head_rel[:, :], cont_rel[:, :], head_ends[:, :], ALU.mult))

        for ph in range(3):
            base, node_base = ph * BNB, ph * BNC
            merge = ALU.add if ph == 0 else ALU.max
            per = BG - 1

            def one_hots(b, q):
                dve.wait_ge(extracted, b + (base + SLOTS - 1))
                v.tensor_scalar(keep_b[:, q, :], keep[:, bass.ds(b, 1), :].rearrange("p b g -> p (b g)"), 0.0, None, ALU.add
                                ).then_inc(keep_copied, 1)
                v.tensor_tensor(hot[:, q], iota1[:, :].unsqueeze(1).to_broadcast([P, BG, P]),
                                end_rel[:, bass.ds(b, 1), :].rearrange("p b g -> p (b g)").unsqueeze(2)
                                .to_broadcast([P, BG, P]), ALU.is_equal)
                v.tensor_scalar(hot_head[:, q, :], iota1[:, :], head_rel[:, bass.ds(b, 1)], None, ALU.is_equal)
                v.tensor_scalar(pass_bc[:, q, :], ones[:, 0:D], passes[:, bass.ds(b, 1)], None, ALU.mult).then_inc(hot_ready, 1)

            def scan(b, q):
                dve.wait_ge(last_T, b + (base + 1))
                dve.wait_ge(row_copied, b + (base + 1))
                if is_int(b, 0):
                    v.memset(held[:, q, 0:1], 0.0).then_inc(held_moved, 1)
                else:
                    v.tensor_scalar(held[:, q, 0:1], held[:, 1 - q, P:P + 1], 0.0, None, ALU.add).then_inc(held_moved, 1)
                dve.wait_ge(held_moved, b + (base + 1))
                v.tensor_tensor_scan(held[:, q, 1:P + 1], pass_row[:, :], ps_last[0:D, 0:P], held[:, q, 0:1],
                                     ALU.mult, merge).then_inc(scanned, 1)
                dve.wait_ge(scanned, b + (base + 1))

            def sum_up(b, q):
                dve.wait_ge(head_copied, b + (base + 1))
                dve.wait_ge(extracted, b + (base + 1 + SLOTS))
                dve.wait_ge(rows_stored, b * 16 + (base * 16 + 16))
                v.tensor_tensor(rows_out[:, q, :], ps_agg[:, 0:D], head_add[:, :], merge).then_inc(rows_ready, 1)

            n_steps = [3, 5, 7][ph]
            base_steps = [0, 3 * BNC, 8 * BNC][ph]

            def node(j):
                at, n = [0], b_size(j)

                def link(ins):
                    at[0] += 1
                    ins.then_inc(node_step, 1)
                    dve.wait_ge(node_step, j * n_steps + (base_steps + at[0]))

                def layer_norm(count):
                    for c in range(n):
                        last = v.bn_stats(bn[:, c, :], t1[:, c, :])
                    link(last)
                    v.memset(scratch[:, 1:2], 0.0)
                    for c in range(n):
                        last = v.bn_aggr(mean_var[:, c, :], bn[:, c, :])
                    last.then_inc(var_in, 1)
                    dve.wait_ge(std_ready, count)
                    link(v.reciprocal(stat[:, 2, 0:n], stat[:, 1, 0:n]))
                    for c in range(n):
                        last = v.tensor_scalar(node_new[:, c, :], t1[:, c, :], mean_var[:, c, 0:1], stat[:, 2, c:c + 1],
                                               ALU.subtract, ALU.mult)
                    last.then_inc(node_ready, 1)

                def l2_scale(count):
                    link(v.tensor_tensor(sq[:, 0:n, :], t2[:, 0:n, :], t2[:, 0:n, :], ALU.mult))
                    v.tensor_reduce(stat[:, 0, 0:n], sq[:, 0:n, :], AX.X, ALU.add).then_inc(var_in, 1)
                    dve.wait_ge(std_ready, count)
                    link(v.tensor_scalar(stat[:, 0, 0:n], stat[:, 1, 0:n], L2_EPS, None, ALU.max))
                    link(v.reciprocal(stat[:, 2, 0:n], stat[:, 0, 0:n]))

                dve.wait_ge(o_ready, j + (node_base + 1))
                halves = [(c0, min(n, c0 + 4), ps_o[c0 // 4]) for c0 in range(0, n, 4)]
                if ph == 0:
                    for c0, c1, bank in halves:
                        last = v.scalar_tensor_tensor(flat(t1[:, c0:c1]), bank[:, 0:(c1 - c0) * D], 0.0,
                                                      flat(res_in[:, c0:c1]), ALU.max, ALU.add)
                    link(last)
                    v.memset(scratch[:, 0:1], 0.0).then_inc(o_used, 1)
                    dve.wait_ge(new_stored, j * 16 + 16)
                    layer_norm(j + 1)
                else:
                    before = t1 if ph == 1 else t2
                    for c0, c1, bank in halves:
                        last = v.tensor_tensor(flat(before[:, c0:c1]), bank[:, 0:(c1 - c0) * D], flat(self_in[:, c0:c1]), ALU.add)
                    link(last)
                    v.memset(scratch[:, 0:1], 0.0).then_inc(o_used, 1)
                    if ph == 1:
                        link(v.tensor_scalar(t2[:, 0:n, :], t1[:, 0:n, :], 0.0, None, ALU.max))
                        l2_scale(j + (BNC + 1))
                        v.tensor_tensor(node_new[:, 0:n, :], t2[:, 0:n, :], stat[:, 2, 0:n].unsqueeze(2).to_broadcast([P, n, D]),
                                        ALU.mult).then_inc(node_ready, 1)
                    else:
                        l2_scale(j * 2 + (2 * BNC + 1))
                        for c in range(n):
                            last = v.scalar_tensor_tensor(t1[:, c, :], t2[:, c, :], stat[:, 2, c:c + 1], res_in[:, c, :],
                                                          ALU.mult, ALU.add)
                        link(last)
                        dve.wait_ge(new_stored, j * 16 + (16 * BNC + 16))
                        layer_norm(j * 2 + (2 * BNC + 2))
                assert at[0] == n_steps
                dve.wait_ge(node_ready, j + (node_base + 1))

            def body(J, k, b):
                q, s = k % 2, k % SLOTS
                one_hots(b, q)
                if not is_int(b, 0):
                    scan(b - 1, 1 - q)
                if not is_int(J, 0) and k == K_SUMS + 1:
                    node(J - 1)
                last = is_int(b, BNB - 1)
                if last:
                    sum_up(b - 1, 1 - q)
                dve.wait_ge(keep_copied, b + (base + 1))
                for g in range(b_steps(b)):
                    if last and g == B_PART:
                        node(BNC - 2)
                    if g in (0, B_PART):
                        h, g1 = (0, B_PART) if g == 0 else (1, b_steps(b))
                        dve.wait_ge(gathered[ph][s][h], b_gathers(J, k, b, h))
                        if ph == 0:
                            dve.wait_ge(w_copied, b * B_NG + (-(-g1 // GQ) + 2))
                            v.tensor_tensor(flat(ring[:, s, g:g1]), w_sb[:, q, g * D:g1 * D],
                                            flat(ring[:, s, g:g1]), ALU.mult).then_inc(msg_done, 1)
                            dve.wait_ge(msg_done, b * 2 + (h + 1))
                    if g:
                        dve.wait_ge(step_done, b * per + (ph * B_STEPS + g))
                        v.scalar_tensor_tensor(ring[:, s, g, :], ring[:, s, g - 1, :], keep_b[:, q, g:g + 1], ring[:, s, g, :],
                                               ALU.mult, merge).then_inc(step_done, 1)
                if not (is_int(b, 0) or last):
                    sum_up(b - 1, 1 - q)


            def tail():
                scan(BNB - 1, 1)
                sum_up(BNB - 1, 1)
                node(BNC - 1)

            turns(dve, body, tail)

    return sync_program, gpsimd_program, tensor_program, scalar_program, vector_program


def build(nc, arrays, out):
    with ExitStack() as ctx:
        def sem(name):
            return ctx.enter_context(nc.semaphore(name))

        bounds_i = ctx.enter_context(nc.sbuf_tensor("bounds_i", [1, BNB + 1], I32))
        bounds_f = ctx.enter_context(nc.sbuf_tensor("bounds_f", [1, BNB + 1], F32))
        width = ctx.enter_context(nc.sbuf_tensor("width", [1, BNB], F32))
        fits = ctx.enter_context(nc.sbuf_tensor("fits", [1, BNB + BT], F32))
        need_i = ctx.enter_context(nc.sbuf_tensor("need_i", [1, BT - 1], I32))
        need = ctx.enter_context(nc.sbuf_tensor("need", [1, BT - 1], F32))
        regular_f = ctx.enter_context(nc.sbuf_tensor("regular_f", [1, 1], F32))
        regular = ctx.enter_context(nc.sbuf_tensor("regular", [1, 1], I32))
        bounds_loaded, need_ready, bound_step, bounds_ready = (sem("bounds_loaded"), sem("need_ready"), sem("bound_step"),
                                                               sem("bounds_ready"))
        shared = {k: arrays[k] for k in ("x_rows", "x_pm", "xT", "w1z", "b1", "w2a", "wsa", "wn", "wpsa")}
        with ExitStack() as memory:
            by_partition = build_by_partition(nc, memory, src=arrays["src"], dst=arrays["dst"], ea=arrays["ea"],
                                              out=out, **shared)
        with ExitStack() as memory:
            by_batch = build_by_batch(nc, memory, bounds_f, bounds_i, bounds_ready, src=arrays["b_src"],
                                      dst=arrays["b_dst"], nxt=arrays["b_nxt"], prv=arrays["b_prv"], ea=arrays["b_ea"],
                                      out=out, **shared)

        def choose(eng, engine):
            eng.wait_ge(bounds_ready, 1)
            flag = eng.value_load(regular[0:1, 0:1], min_val=0, max_val=1)
            with eng.If(flag != 0):
                by_batch[engine](eng)
            with eng.Else():
                by_partition[engine](eng)

        block = ctx.enter_context(nc.Block())

        @block.sync
        def _(sp):
            sp.dma_start(bounds_i[:, 0:BNB], arrays["b_first"]).then_inc(bounds_loaded, 16)
            choose(sp, 0)

        @block.gpsimd
        def _(pool):
            pool.iota(need_i[:, :], [[C * P, BT - 1]], base=C * P, channel_multiplier=0).then_inc(need_ready, 1)
            choose(pool, 1)

        @block.tensor
        def _(pe):
            choose(pe, 2)

        @block.scalar
        def _(act):
            choose(act, 3)

        @block.vector
        def _(dve):
            v = nc.vector
            done = [0]

            def chain(ins):
                done[0] += 1
                ins.then_inc(bound_step, 1)
                dve.wait_ge(bound_step, done[0])

            dve.wait_ge(bounds_loaded, 16)
            dve.wait_ge(need_ready, 1)
            chain(v.memset(bounds_i[:, 0:1], 0))
            v.tensor_copy(bounds_f[:, 0:BNB], bounds_i[:, 0:BNB])
            v.memset(bounds_f[:, BNB:BNB + 1], float(N))
            chain(v.tensor_copy(need[:, :], need_i[:, :]))
            chain(v.tensor_tensor(width[:, :], bounds_f[:, 1:BNB + 1], bounds_f[:, 0:BNB], ALU.subtract))
            v.tensor_scalar(fits[:, 0:BNB], width[:, :], float(P), None, ALU.is_le)
            chain(v.tensor_tensor(fits[:, BNB:BNB + BT - 1], bounds_f[:, K + 1:BNB:K], need[:, :], ALU.is_ge))
            chain(v.tensor_scalar(fits[:, BNB + BT - 1:BNB + BT], bounds_f[:, B_DONE + 1:B_DONE + 2],
                                  float((NBLK - B_SIZES[-1]) * P), None, ALU.is_ge))
            chain(v.tensor_reduce(regular_f[:, :], fits[:, :], AX.X, ALU.min))
            v.tensor_copy(regular[:, :], regular_f[:, :]).then_inc(bounds_ready, 1)
            choose(dve, 4)


def kernel(**inputs):
    from concourse import bacc
    from concourse.bass_utils import run_bass_kernel_spmd

    a = {k: np.asarray(v) for k, v in inputs.items()}
    f32, i32 = np.float32, np.int32

    def rows(x, n, fill=0):
        pad = np.full((n - x.shape[0],) + x.shape[1:], fill, x.dtype)
        return np.concatenate([x, pad])

    def steps(x):
        x = x.reshape((P, T) + x.shape[1:])
        return np.concatenate([x, np.zeros((P, NB * G - T) + x.shape[2:], x.dtype)], 1)

    src = steps(rows(a["src"], EP))
    dst = rows(a["dst"], EP, NP).reshape(P, T)
    ea = steps(rows(a["edge_attr_17"], EP)).reshape(P, NB, NG, GQ, ED).transpose(2, 4, 1, 3, 0).reshape(NG * ED, NB, GQ * P)
    x = rows(a["x"], NP)
    x_pm = x.reshape(NBLK, P, D).transpose(1, 0, 2).reshape(P, NBLK * D)
    w1z = np.zeros((NG * ED, NG, D), f32)
    for g in range(NG):
        w1z[g * ED:(g + 1) * ED, g] = a["L0_gnn_W1"].T
    w2a = np.concatenate([a["L0_gnn_W2"].T, a["L0_gnn_b2"][None]])
    wsa = np.concatenate([a["L0_gnn_Ws"].T, a["L0_gnn_bs"][None], a["L0_gnn_bn"][None]])
    wn = np.stack([a["L0_gnn_Wn"].T, a["L1_gnn_Wn1"], a["L1_gnn_Wn2"]], 1)
    def shifted(x, by, before, after):
        return np.concatenate([[before], x, [after]]).astype(x.dtype)[1 + by:1 + by + len(x)]

    def by_batch(x):
        full, last = np.split(x, [(BNB - 1) * BE])
        full = full.reshape((BNB - 1, P, BG) + x.shape[1:])
        last = last.reshape((1, P, BGL) + x.shape[1:])
        last = np.concatenate([last, np.repeat(last[:, :, -1:], BG - BGL, 2)], 2)
        return np.concatenate([full, last]).swapaxes(0, 1).reshape((P, BNB * BG) + x.shape[1:])

    b_dst = rows(a["dst"], BEP, NP)
    b_ea = np.concatenate([by_batch(rows(a["edge_attr_17"], BEP)).reshape(P, BNB, BG, ED),
                           np.zeros((P, BNB, B_NG * GQ - BG, ED), f32)], 2)
    b_ea = b_ea.reshape(P, BNB, B_NG, GQ, ED).transpose(2, 4, 1, 3, 0).reshape(B_NG * ED, BNB, GQ * P)
    wpsa = np.stack([np.concatenate([np.concatenate([a[f"L1_gnn_Wp{n}"], a[f"L1_gnn_bp{n}"][None]]),
                                     np.concatenate([a[f"L1_gnn_Ws{n}"], a[f"L1_gnn_b{n}"][None]])], 1) for n in (1, 2)], 1)
    arrays = {"src": src, "dst": dst, "ea": ea, "x_pm": x_pm, "xT": rows(x, TURNS * CS * P).T, "w1z": w1z,
              "b1": a["L0_gnn_b1"][:, None], "w2a": w2a, "wsa": wsa, "wn": wn, "wpsa": wpsa, "x_rows": x,
              "b_first": b_dst[None, ::BE], "b_src": by_batch(rows(a["src"], BEP)), "b_dst": by_batch(b_dst),
              "b_nxt": by_batch(shifted(b_dst, 1, -1, NP)), "b_prv": by_batch(shifted(b_dst, -1, -1, NP)), "b_ea": b_ea}
    arrays = {k: np.ascontiguousarray(v) for k, v in arrays.items()}
    nc = bacc.Bacc("TRN2", target_bir_lowering=False, num_devices=1)
    aps = {k: nc.dram_tensor(k, v.shape, mybir.dt.from_np(v.dtype), kind="ExternalInput").ap() for k, v in arrays.items()}
    out = nc.dram_tensor("out", (P, NBLK * D), F32, kind="ExternalOutput").ap()
    build(nc, aps, out)
    r = run_bass_kernel_spmd(nc, [arrays], core_ids=[0])
    got = np.asarray(r.results[0]["out"])
    return got.reshape(P, NBLK, D).transpose(1, 0, 2).reshape(NP, D)[:N]
```
